# Optimizing a Trainium2 kernel written in Bass

```python
import numpy as np
import jax
import jax.numpy as jnp

def _softmax(x, axis=-1):
    return jax.nn.softmax(x, axis=axis)

def _gelu(x):
    return jax.nn.gelu(x, approximate=True)

def _silu(x):
    return jax.nn.silu(x)

def _sigmoid(x):
    return jax.nn.sigmoid(x)

def _layernorm(x, axis=-1, eps=1e-05):
    m = jnp.mean(x, axis=axis, keepdims=True)
    v = jnp.var(x, axis=axis, keepdims=True)
    return (x - m) / jnp.sqrt(v + eps)

def _scatter_add(tgt, idx, src, axis=0):
    return tgt.at[idx].add(src)

def _segment_sum(src, seg, n):
    return jax.ops.segment_sum(src, seg, n)
kernel_name = 'mk_cond_resid_d2_seqx_r4_679dba'

def setup_inputs(seed: int=0):
    np.random.seed(seed)
    _w = jnp.asarray

    def _rec_inputs():
        import jax
        import jax.numpy as jnp
        _rk = jax.random.key(seed)
        x = 7.22e-05 + 1 * jax.random.normal(jax.random.fold_in(_rk, 1), (4, 512, 256), jnp.float32)
        _lenS = 512 - jax.random.randint(jax.random.fold_in(_rk, 7), (4,), 0, max(1, 512 // 4) + 1, jnp.int32)
        _lenS2 = 512 - jax.random.randint(jax.random.fold_in(_rk, 8), (4,), 0, max(1, 512 // 4) + 1, jnp.int32)
        cond_64 = -0.104238 + 1.01173 * jax.random.normal(jax.random.fold_in(_rk, 11), (4, 64), jnp.float32)
        fside_16xSxS_0 = -5.72187e-05 + 0.999849 * jax.random.normal(jax.random.fold_in(_rk, 12), (16, 512, 512), jnp.float32)
        _validS = jnp.arange(512)[None, :] < _lenS[:, None]
        _validS2 = jnp.arange(512)[None, :] < _lenS2[:, None]
        _causal = jnp.tril(jnp.ones((512, 512), dtype=bool))
        mask_BxS_bk0 = jnp.logical_not(jnp.broadcast_to(_validS[:, :], (4, 512)))
        return (x, cond_64, fside_16xSxS_0, mask_BxS_bk0)
    x, cond_64, fside_16xSxS_0, mask_BxS_bk0 = _rec_inputs()

    def _L0_cond_setup():
        import jax, jax.numpy as jnp
        import numpy as np
        B, S, H = (4, 512, 256)
        E = 8
        M = 128
        K = 2
        N_SHARED = 2
        SM = M * N_SHARED
        G = 64
        GE_TEMP = 1.0
        ALPHA = 0.001
        SEQ_AUX = True
        NORM_TOPK = True
        COS_TEMP = 0.78
        CONS_ALPHA = 0.01
        LEAKY_SLOPE = 0.01
        EPS_COS = 1e-08

        def _leaky(x):
            return jnp.where(x >= 0, x, LEAKY_SLOPE * x)

        def _moe_forward(hidden_states, g, wt, wg, w_gate, w_up, w_down, sw_gate, sw_up, sw_down):
            b, s, h = hidden_states.shape
            x = hidden_states.reshape(-1, h)
            T = x.shape[0]
            logits_h = x @ wt.T
            logits_g = g @ wg.T
            logits_g = jnp.repeat(logits_g, s, axis=0)
            logits = (logits_h + logits_g / GE_TEMP) / (1.0 + 1.0 / GE_TEMP)
            scores = jax.nn.softmax(logits, axis=-1)
            topk_w, topk_idx = jax.lax.top_k(scores, K)
            if K > 1 and NORM_TOPK:
                topk_w = topk_w / (topk_w.sum(-1, keepdims=True) + 1e-20)
            onehot = jax.nn.one_hot(topk_idx.reshape(b, s * K), E, dtype=jnp.float32)
            ce = onehot.sum(1) / (s * K / E)
            aux_loss = (ce * scores.reshape(b, s, E).mean(1)).sum(1).mean() * ALPHA
            gp = _leaky(jnp.einsum('th,ehm->etm', x, w_gate))
            up = jnp.einsum('th,ehm->etm', x, w_up)
            y_all = jnp.einsum('etm,emh->eth', gp * up, w_down)
            y_sel = y_all[topk_idx, jnp.arange(T)[:, None], :]
            y = (y_sel * topk_w[..., None]).sum(1).reshape(b, s, h)
            p = _leaky(hidden_states @ sw_gate) * (hidden_states @ sw_up) @ sw_down
            y = y + p
            num = jnp.sum(y * p, -1)
            den = jnp.maximum(jnp.linalg.norm(y, axis=-1), EPS_COS) * jnp.maximum(jnp.linalg.norm(p, axis=-1), EPS_COS)
            closs = CONS_ALPHA * jnp.mean(num / den / (1.0 + COS_TEMP))
            return (y, aux_loss + closs)
        key = jax.random.key(seed)
        ks = jax.random.split(key, 12)
        sh = 1.0 / np.sqrt(H)
        sm = 1.0 / np.sqrt(M)
        ssm = 1.0 / np.sqrt(SM)
        sg = 1.0 / np.sqrt(G)
        return {'hidden_states': jax.random.normal(ks[0], (B, S, H), jnp.float32), 'g': jax.random.normal(ks[1], (B, G), jnp.float32), 'wt': jax.random.uniform(ks[2], (E, H), jnp.float32, -sh, sh), 'wg': jax.random.uniform(ks[3], (E, G), jnp.float32, -sg, sg), 'w_gate': jax.random.uniform(ks[4], (E, H, M), jnp.float32, -sh, sh), 'w_up': jax.random.uniform(ks[5], (E, H, M), jnp.float32, -sh, sh), 'w_down': jax.random.uniform(ks[6], (E, M, H), jnp.float32, -sm, sm), 'sw_gate': jax.random.uniform(ks[7], (H, SM), jnp.float32, -sh, sh), 'sw_up': jax.random.uniform(ks[8], (H, SM), jnp.float32, -sh, sh), 'sw_down': jax.random.uniform(ks[9], (SM, H), jnp.float32, -ssm, ssm)}
    _L0_cond_all = _L0_cond_setup()
    _L0_cond_in = {k: v for k, v in _L0_cond_all.items() if k in ('wt', 'wg', 'w_gate', 'w_up', 'w_down', 'sw_gate', 'sw_up', 'sw_down')}
    del _L0_cond_all

    def _L1_cond_setup():
        import jax, jax.numpy as jnp
        import numpy as np
        B, N, DIM, H, DH = (2, 512, 256, 16, 64)
        INNER = H * DH
        EPS = 1e-05

        def layernorm(x, g):
            mean = jnp.mean(x, axis=-1, keepdims=True)
            var = jnp.var(x, axis=-1, keepdims=True)
            return (x - mean) * jax.lax.rsqrt(var + EPS) * g
        key = jax.random.key(seed)
        ks = jax.random.split(key, 10)
        x = jax.random.normal(ks[0], (B, N, DIM), dtype=jnp.float32)
        attn_bias = jax.random.normal(ks[1], (H, N, N), dtype=jnp.float32)
        mask = jax.random.randint(ks[2], (B, N), 0, 2).astype(bool)
        g_in = jnp.ones((DIM,), dtype=jnp.float32)
        null_attn_bias = jax.random.normal(ks[3], (H,), dtype=jnp.float32)
        null_kv = jax.random.normal(ks[4], (2, DH), dtype=jnp.float32)
        Wq = jax.random.normal(ks[5], (DIM, INNER), dtype=jnp.float32) * 0.02
        Wkv = jax.random.normal(ks[6], (DIM, 2 * DH), dtype=jnp.float32) * 0.02
        Wo = jax.random.normal(ks[7], (INNER, DIM), dtype=jnp.float32) * 0.02
        g_out = jnp.ones((DIM,), dtype=jnp.float32)
        return {'x': x, 'attn_bias': attn_bias, 'mask': mask, 'g_in': g_in, 'null_attn_bias': null_attn_bias, 'null_kv': null_kv, 'Wq': Wq, 'Wkv': Wkv, 'Wo': Wo, 'g_out': g_out}
    _L1_cond_all = _L1_cond_setup()
    _L1_cond_in = {k: v for k, v in _L1_cond_all.items() if k in ('g_in', 'null_attn_bias', 'Wq', 'Wkv', 'Wo', 'g_out')}
    del _L1_cond_all
    return {'x': x, 'cond_64': cond_64, 'fside_16xSxS_0': fside_16xSxS_0, 'mask_BxS_bk0': mask_BxS_bk0, 'L0_cond_wt': _L0_cond_in['wt'], 'L0_cond_wg': _L0_cond_in['wg'], 'L0_cond_w_gate': _L0_cond_in['w_gate'], 'L0_cond_w_up': _L0_cond_in['w_up'], 'L0_cond_w_down': _L0_cond_in['w_down'], 'L0_cond_sw_gate': _L0_cond_in['sw_gate'], 'L0_cond_sw_up': _L0_cond_in['sw_up'], 'L0_cond_sw_down': _L0_cond_in['sw_down'], 'L1_cond_g_in': _L1_cond_in['g_in'], 'L1_cond_null_attn_bias': _L1_cond_in['null_attn_bias'], 'L1_cond_Wq': _L1_cond_in['Wq'], 'L1_cond_Wkv': _L1_cond_in['Wkv'], 'L1_cond_Wo': _L1_cond_in['Wo'], 'L1_cond_g_out': _L1_cond_in['g_out']}

def reference(x, cond_64, fside_16xSxS_0, mask_BxS_bk0, L0_cond_wt, L0_cond_wg, L0_cond_w_gate, L0_cond_w_up, L0_cond_w_down, L0_cond_sw_gate, L0_cond_sw_up, L0_cond_sw_down, L1_cond_g_in, L1_cond_null_attn_bias, L1_cond_Wq, L1_cond_Wkv, L1_cond_Wo, L1_cond_g_out):
    import jax
    import jax.numpy as jnp

    def _L0_cond_ref(hidden_states, g, wt, wg, w_gate, w_up, w_down, sw_gate, sw_up, sw_down):
        import jax, jax.numpy as jnp
        import numpy as np
        B, S, H = (4, 512, 256)
        E = 8
        M = 128
        K = 2
        N_SHARED = 2
        SM = M * N_SHARED
        G = 64
        GE_TEMP = 1.0
        ALPHA = 0.001
        SEQ_AUX = True
        NORM_TOPK = True
        COS_TEMP = 0.78
        CONS_ALPHA = 0.01
        LEAKY_SLOPE = 0.01
        EPS_COS = 1e-08

        def _leaky(x):
            return jnp.where(x >= 0, x, LEAKY_SLOPE * x)

        def _moe_forward(hidden_states, g, wt, wg, w_gate, w_up, w_down, sw_gate, sw_up, sw_down):
            b, s, h = hidden_states.shape
            x = hidden_states.reshape(-1, h)
            T = x.shape[0]
            logits_h = x @ wt.T
            logits_g = g @ wg.T
            logits_g = jnp.repeat(logits_g, s, axis=0)
            logits = (logits_h + logits_g / GE_TEMP) / (1.0 + 1.0 / GE_TEMP)
            scores = jax.nn.softmax(logits, axis=-1)
            topk_w, topk_idx = jax.lax.top_k(scores, K)
            if K > 1 and NORM_TOPK:
                topk_w = topk_w / (topk_w.sum(-1, keepdims=True) + 1e-20)
            onehot = jax.nn.one_hot(topk_idx.reshape(b, s * K), E, dtype=jnp.float32)
            ce = onehot.sum(1) / (s * K / E)
            aux_loss = (ce * scores.reshape(b, s, E).mean(1)).sum(1).mean() * ALPHA
            gp = _leaky(jnp.einsum('th,ehm->etm', x, w_gate))
            up = jnp.einsum('th,ehm->etm', x, w_up)
            y_all = jnp.einsum('etm,emh->eth', gp * up, w_down)
            y_sel = y_all[topk_idx, jnp.arange(T)[:, None], :]
            y = (y_sel * topk_w[..., None]).sum(1).reshape(b, s, h)
            p = _leaky(hidden_states @ sw_gate) * (hidden_states @ sw_up) @ sw_down
            y = y + p
            num = jnp.sum(y * p, -1)
            den = jnp.maximum(jnp.linalg.norm(y, axis=-1), EPS_COS) * jnp.maximum(jnp.linalg.norm(p, axis=-1), EPS_COS)
            closs = CONS_ALPHA * jnp.mean(num / den / (1.0 + COS_TEMP))
            return (y, aux_loss + closs)
        y, _ = _moe_forward(hidden_states, g, wt, wg, w_gate, w_up, w_down, sw_gate, sw_up, sw_down)
        return y

    def _L1_cond_ref(x, attn_bias, mask, g_in, null_attn_bias, null_kv, Wq, Wkv, Wo, g_out):
        import jax, jax.numpy as jnp
        import numpy as np
        B, N, DIM, H, DH = (2, 512, 256, 16, 64)
        INNER = H * DH
        EPS = 1e-05

        def layernorm(x, g):
            mean = jnp.mean(x, axis=-1, keepdims=True)
            var = jnp.var(x, axis=-1, keepdims=True)
            return (x - mean) * jax.lax.rsqrt(var + EPS) * g
        b, n, _ = x.shape
        scale = DH ** (-0.5)
        xn = layernorm(x, g_in)
        q = (xn @ Wq).reshape(b, n, H, DH).transpose(0, 2, 1, 3) * scale
        kv = xn @ Wkv
        k, v = (kv[..., :DH], kv[..., DH:])
        nk = jnp.broadcast_to(null_kv[0], (b, 1, DH))
        nv = jnp.broadcast_to(null_kv[1], (b, 1, DH))
        k = jnp.concatenate([nk, k], axis=1)
        v = jnp.concatenate([nv, v], axis=1)
        sim = jnp.einsum('bhid,bjd->bhij', q, k)
        null_col = jnp.broadcast_to(null_attn_bias[:, None, None], (H, n, 1))
        bias = jnp.concatenate([null_col, attn_bias], axis=-1)
        sim = sim + bias
        neg = -jnp.finfo(sim.dtype).max
        j = n + 1
        causal_mask = jnp.triu(jnp.ones((n, j), dtype=bool), k=j - n + 1)
        sim = jnp.where(causal_mask, neg, sim)
        mask_p = jnp.pad(mask, ((0, 0), (1, 0)), constant_values=True)
        sim = jnp.where(mask_p[:, None, None, :], sim, neg)
        attn = jax.nn.softmax(sim, axis=-1)
        out = jnp.einsum('bhij,bjd->bhid', attn, v)
        out = out.transpose(0, 2, 1, 3).reshape(b, n, INNER)
        out = out @ Wo
        return layernorm(out, g_out)
    x = x + _L0_cond_ref(x, cond_64, L0_cond_wt, L0_cond_wg, L0_cond_w_gate, L0_cond_w_up, L0_cond_w_down, L0_cond_sw_gate, L0_cond_sw_up, L0_cond_sw_down)
    x = x + _L1_cond_ref(x, fside_16xSxS_0, mask_BxS_bk0, L1_cond_g_in, L1_cond_null_attn_bias, cond_64, L1_cond_Wq, L1_cond_Wkv, L1_cond_Wo, L1_cond_g_out)
    return x

_drawn_inputs = setup_inputs


def setup_inputs(seed=0):
    import zlib

    import numpy as np

    out = dict(_drawn_inputs(seed))
    spreads = {'L1_cond_g_in': (1.0, 0.2), 'L1_cond_g_out': (1.0, 0.2)}
    factors = {}
    for name, (base, spread) in spreads.items():
        noise = np.random.default_rng([zlib.crc32(name.encode()), seed]).standard_normal(out[name].shape)
        drawn = base * np.exp(spread * noise) if base else spread * noise
        out[name] = jnp.asarray(drawn.astype(out[name].dtype))
    for name, factor in factors.items():
        out[name] = (out[name] * factor).astype(out[name].dtype)
    return out
```

```python
from contextlib import ExitStack

import concourse.bass as bass
from concourse import mybir

P = 128
F32 = mybir.dt.float32
F32R = mybir.dt.float32r
BF16 = mybir.dt.bfloat16
U8 = mybir.dt.uint8
I32 = mybir.dt.int32
ALU = mybir.AluOpType
ACT = mybir.ActivationFunctionType
AX_X = mybir.AxisListType.X
AX_XY = mybir.AxisListType.XY

BIG = 1e30
EPS = 1e-5
LEAK = 0.01
CREDIT = 2


def moe_then_attention(nc, x, cond, fside, mask, wt, wg, w_gate, w_up, w_down, sw_gate, sw_up, sw_down,
                       g_in, null_bias, w_q, w_kv, w_o, g_out, out):
    NB, S, H = x.shape
    E = w_gate.shape[0]
    M = w_gate.shape[2]
    NSH = sw_gate.shape[1] // M
    NU = NSH + E
    G = cond.shape[1]
    NH = fside.shape[0]
    INNER = w_q.shape[1]
    DH = INNER // NH
    KB = H // P
    QT = S // P
    NT = NB * QT
    PAIRS = NH // 2
    HG = 4
    NG = NH // HG
    D1 = DH + 1
    NW = NB * NG
    assert M == P and S == 512 and KB == 2 and DH == 64 and NB == 4 and NSH == 2 and NU % 2 == 0 and G == DH

    with ExitStack() as ctx:
        def sb(name, shape, dt=F32):
            return ctx.enter_context(nc.sbuf_tensor(name, shape, dt))

        def sem(name):
            return ctx.enter_context(nc.semaphore(name))

        bank = [ctx.enter_context(nc.psum_tensor(f"bank{i}", [P, 512], F32)) for i in range(8)]
        gate_ps, up_ps, wb_ps, y_ps, misc_ps = bank[0:2], bank[2:4], bank[4], bank[5:7], bank[7]
        logit_ps, pt_ps, pv_ps, proj_ps = bank[0:2], bank[2:4], bank[5:7], (bank[4], bank[7])

        xtok = sb("xtok", [P, NT, H])
        xtf = sb("xtf", [P, 2, KB, S])
        xth = sb("xth", [P, KB, NB * S], F32R)
        xtl = sb("xtl", [P, KB, NB * S], F32R)
        wraw = sb("wraw", [P, NU * 3 * 256])
        wqh = sb("wqh", [P, KB, INNER], F32R)
        wql = sb("wql", [P, KB, INNER], F32R)
        wkvh = sb("wkvh", [P, KB, 3 * DH], F32R)
        wkvl = sb("wkvl", [P, KB, 3 * DH], F32R)
        wo = sb("wo", [P, PAIRS, H])
        hid = sb("hid", [P, 2, S])
        huh = sb("huh", [P, 2, S], F32R)
        hul = sb("hul", [P, 2, S], F32R)
        obuf = sb("obuf", [P, QT, H])
        ident = sb("ident", [P, P])
        identb = sb("identb", [P, P], BF16)
        small = hid[0:8, 1, :]
        wtT = sb("wtT", [P, KB, 8])
        wgT = sb("wgT", [G, 8])
        condT = sb("condT", [P, 4])
        gcol = hid[0:G, 0, :].rearrange("p (b t) -> p b t", b=NB)
        nkz = sb("nkz", [P, 2])
        nvc = sb("nvc", [P, P])
        nv1 = sb("nv1", [P, D1])
        nbias = sb("nbias", [P, NH])
        gin = sb("gin", [P, KB])
        gout = sb("gout", [P, H])
        oc = sb("oc", [P, H])
        masku = obuf[0:1, 2:4, :].rearrange("p t h -> p (t h)").bitcast(U8)
        maskb = sb("maskb", [1, NB * S], BF16)
        onesb = sb("onesb", [1, P], BF16)
        live4 = sb("live4", [1, QT])
        pow2 = sb("pow2", [1, QT])
        livew = sb("livew", [1, 1])
        livei = sb("livei", [1, 1], I32)
        rt = [obuf[:, i // 2, (i % 2) * NT * E:(i % 2 + 1) * NT * E].rearrange("p (t e) -> p t e", e=E)
              for i in range(4)]
        r1 = [sb(f"r1{i}", [P, NT, 1]) for i in range(4)]
        desc = sb("desc", [P, NT, E])
        w3 = sb("w3", [P, NT, 3, E], BF16)
        w3t = sb("w3t", [3 * E, NT * P], BF16)
        sel = sb("sel", [3 * E, E, P], BF16)
        st6 = sb("st6", [P, QT, 6])
        mv = sb("mv", [P, QT, 2])
        rstd = sb("rstd", [P, QT])
        half = sb("half", [P, QT])
        mx = sb("mx", [P, NH])
        mstate = sb("mstate", [P, NB, NH])
        dm = sb("dm", [P, 2, NH])
        alpha = sb("alpha", [P, 2, NH])
        rl = sb("rl", [P, NB, NH])
        nop1 = sb("nop1", [1, 1])

        with ExitStack() as early:
            wh = early.enter_context(nc.sbuf_tensor("wh", [P, NU, 3, 256], F32R))
            wl = early.enter_context(nc.sbuf_tensor("wl", [P, NU, 3, 256], F32R))
        qt_sb = sb("qt_sb", [P, PAIRS, NB, P])
        ost = sb("ost", [P, NB, NH, D1])
        kz = sb("kz", [P, NB, 2, P])
        vt = sb("vt", [DH, NB, P])
        v1 = sb("v1", [P, NB, D1])
        ssb = sb("ssb", [P, 2, NH, P])
        pt = sb("pt", [P, 2, HG, P])

        yt = xtf[:, 0, :, :]
        xn = xtf[:, 1, :, :].rearrange("p k (t h) -> p (k t) h", h=H)
        wraw_u = wraw[:, :].rearrange("p (u w n) -> p u w n", u=NU, w=3)
        bias = wraw[:, 0:NH * P].rearrange("p (h k) -> p h k", h=NH)
        wq_raw = wraw[:, NH * P:NH * P + KB * INNER].rearrange("p (k n) -> p k n", k=KB)
        wkv_raw = wraw[:, NH * P + KB * INNER:NH * P + KB * INNER + KB * 3 * DH].rearrange("p (k n) -> p k n", k=KB)
        xth_q = xth[:, :, :].rearrange("p k (b s) -> p k b s", b=NB)
        xtl_q = xtl[:, :, :].rearrange("p k (b s) -> p k b s", b=NB)
        xtok_q = xtok[:, :, :].rearrange("p (b t) h -> p b t h", b=NB)
        mask_q = maskb[:, :].rearrange("o (b s) -> o b s", b=NB)
        out_q = out.rearrange("b (t p) h -> b p t h", p=P)

        x_in = [sem(f"x_in{b}") for b in range(NB)]
        small_in = sem("small_in")
        w_in = [sem(f"w_in{i}") for i in range(1 + E // 2)]
        wq_in = sem("wq_in")
        wo_in = sem("wo_in")
        vec_in = sem("vec_in")
        mask_in = sem("mask_in")
        zeroed = sem("zeroed")
        consts = sem("consts")
        small_tr = sem("small_tr")
        small_ev = sem("small_ev")
        xt_tr = sem("xt_tr")
        xt_ev = sem("xt_ev")
        xt_high = sem("xt_high")
        xt_low = sem("xt_low")
        routed = sem("routed")
        dve_chain = sem("dve_chain")
        pool_chain = sem("pool_chain")
        w3_ready = sem("w3_ready")
        w3_tr = sem("w3_tr")
        w3_ev = sem("w3_ev")
        wh_done = sem("wh_done")
        wl_done = sem("wl_done")
        wqh_done = sem("wqh_done")
        wql_done = sem("wql_done")
        live_done = sem("live_done")
        g_ready = sem("g_ready")
        g_free = sem("g_free")
        u_ready = sem("u_ready")
        u_free = sem("u_free")
        wb_ready = sem("wb_ready")
        wb_free = sem("wb_free")
        leaked = sem("leaked")
        huh_done = sem("huh_done")
        hul_done = sem("hul_done")
        down_done = sem("down_done")
        y_free = sem("y_free")
        m_ready = sem("m_ready")
        m_free = sem("m_free")
        oc_ready = sem("oc_ready")
        oc_stat = sem("oc_stat")
        oc_mv = sem("oc_mv")
        oc_rstd = sem("oc_rstd")
        oc_norm = sem("oc_norm")
        oc_done = sem("oc_done")
        st_done = sem("st_done")
        mv_done = sem("mv_done")
        rstd_done = sem("rstd_done")
        xn_done = sem("xn_done")
        xnh_done = sem("xnh_done")
        xnl_done = sem("xnl_done")
        ob_ready = sem("ob_ready")
        ob_out = sem("ob_out")
        tiles_set = sem("tiles_set")
        q_ready = sem("q_ready")
        q_evac = sem("q_evac")
        null_ready = sem("null_ready")
        m_init = sem("m_init")
        o_init = sem("o_init")
        bias_in = sem("bias_in")
        bias_masked = sem("bias_masked")
        kv_ready = sem("kv_ready")
        kv_evac = sem("kv_evac")
        v_ready = sem("v_ready")
        v_evac = sem("v_evac")
        s_ready = sem("s_ready")
        s_added = sem("s_added")
        s_max = sem("s_max")
        m_delta = sem("m_delta")
        m_new = sem("m_new")
        m_step = sem("m_step")
        s_shift = sem("s_shift")
        alpha_done = sem("alpha_done")
        p_done = sem("p_done")
        pt_ready = sem("pt_ready")
        pt_evac = sem("pt_evac")
        pv_ready = sem("pv_ready")
        o_scaled = sem("o_scaled")
        o_added = sem("o_added")
        rl_done = sem("rl_done")
        on_done = sem("on_done")
        ot_ready = sem("ot_ready")
        ot_evac = sem("ot_evac")
        wo_ready = sem("wo_ready")
        ln_stat = sem("ln_stat")
        ln_mv = sem("ln_mv")
        ln_rstd = sem("ln_rstd")
        ln_eps = sem("ln_eps")
        ln_norm = sem("ln_norm")
        ln_scale = sem("ln_scale")
        row_done = sem("row_done")
        row_out = sem("row_out")
        passed = sem("passed")

        block = ctx.enter_context(nc.Block())

        UNIT_IN = [0] * NSH + [1 + e // 2 for e in range(E)]
        OC_M = 2
        TOT = NB * NU

        primed = (s_added, pt_ready, wo_ready, alpha_done, o_added, on_done, ln_norm, v_evac, pt_evac, row_out,
                  ob_out)

        def wait_apart(eng, semaphore, value):
            eng.wait_ge(semaphore, value)
            eng.sem_inc(passed, 1)

        def split3(mm, acc, wa, wb_, ra, rb, first, last):
            mm(acc, wa, ra, start=first, stop=False)
            mm(acc, wa, rb, start=False, stop=False)
            return mm(acc, wb_, ra, start=False, stop=last)

        @block.sync
        def _(sp):
            for semaphore in primed:
                sp.sem_inc(semaphore, 1)
            sp.dma_start(xtok[:, 0:QT, :], x[0].rearrange("(t p) h -> p t h", p=P)).then_inc(x_in[0], 16)
            for kind, src in ((0, sw_gate), (1, sw_up)):
                for u in range(NSH):
                    sp.dma_start(wraw_u[:, u, kind, :].rearrange("p (k m) -> p k m", k=KB),
                                 src.rearrange("(k p) (u m) -> u p k m", p=P, u=NSH)[u]).then_inc(w_in[0], 16)
            sp.dma_start(wraw_u[:, 0:NSH, 2, :], sw_down.rearrange("(u p) h -> p u h", p=P)).then_inc(w_in[0], 16)
            sp.dma_start(xtok[:, QT:2 * QT, :], x[1].rearrange("(t p) h -> p t h", p=P)).then_inc(x_in[1], 16)
            for i in range(E // 2):
                for e in (2 * i, 2 * i + 1):
                    for kind, src in ((0, w_gate), (1, w_up)):
                        sp.dma_start(wraw_u[:, NSH + e, kind, :].rearrange("p (k m) -> p k m", k=KB),
                                     src[e].rearrange("(k p) m -> p k m", p=P)).then_inc(w_in[1 + i], 16)
                    sp.dma_start(wraw_u[:, NSH + e, 2, :], w_down[e]).then_inc(w_in[1 + i], 16)
                if i < 2:
                    sp.dma_start(xtok[:, (2 + i) * QT:(3 + i) * QT, :],
                                 x[2 + i].rearrange("(t p) h -> p t h", p=P)).then_inc(x_in[2 + i], 16)
            sp.dma_start(wo[:, :, :], w_o.rearrange("(j p) h -> p j h", p=P)).then_inc(wo_in, 16)
            sp.wait_ge(wh_done, NU)
            sp.wait_ge(wl_done, NU)
            sp.dma_start(wq_raw, w_q.rearrange("(k p) n -> p k n", p=P)).then_inc(wq_in, 16)
            kvr = w_kv.rearrange("(k p) n -> p k n", p=P)
            sp.dma_start(wkv_raw[:, :, 0:DH], kvr[:, :, DH:2 * DH]).then_inc(wq_in, 16)
            sp.dma_start(wkv_raw[:, :, DH:2 * DH], kvr[:, :, 0:DH]).then_inc(wq_in, 16)
            sp.dma_start(wkv_raw[:, :, 2 * DH:3 * DH], kvr[:, :, 0:DH]).then_inc(wq_in, 16)

            with sp.Fori(0, NB) as b:
                sp.wait_ge(ob_ready, b + 1)
                sp.dma_start(out_q[b], obuf[:, :, :]).then_inc(ob_out, 16)
            sp.wait_ge(ob_out, 1 + 16 * NB)
            sp.wait_ge(live_done, 1)
            live = sp.value_load(livei[0:1, 0:1], min_val=0, max_val=2 ** QT - 1)
            jobs = sp.alloc_register("sp_jobs")
            tiles = sp.alloc_register("sp_tiles")
            sp.reg_mov(jobs, 0)
            sp.reg_mov(tiles, 0)
            with sp.Fori(0, QT) as q:
                with sp.If((live & ((2 << q) - 1)) > 0):
                    with sp.Fori(0, q + 1) as k:
                        with sp.If(((live >> k) & 1) > 0):
                            j = sp.snap(jobs, min_val=0, max_val=QT * QT)
                            sp.wait_ge(s_added, 1 + j * NW)
                            sp.dma_start(bias, fside[:, bass.ds(q * P, P), bass.ds(k * P, P)]
                                         .rearrange("h p k -> p h k")).then_inc(bias_in, 16)
                            sp.reg_add(jobs, jobs, 1)
                    t = sp.snap(tiles, min_val=0, max_val=QT)
                    for b in range(NB):
                        sp.wait_ge(row_done, t * NB + b + 1)
                        sp.dma_start(out_q[b][:, bass.ds(q, 1), :], obuf[:, b:b + 1, :]).then_inc(row_out, 16)
                    wait_apart(sp, row_out, 1 + t * (16 * NB) + 16 * NB)
                    sp.reg_add(tiles, tiles, 1)

        @block.gpsimd
        def _(pool):
            def link(ins, n=[0]):
                n[0] += 1
                ins.then_inc(pool_chain, 1)
                pool.wait_ge(pool_chain, n[0])

            pool.memset(ident[:, :], 0.0).then_inc(zeroed, 1)
            pool.memset(identb[:, :], 0.0).then_inc(zeroed, 1)
            pool.memset(sel[:, :, :], 0.0).then_inc(zeroed, 1)
            pool.wait_ge(zeroed, 3)
            for m in (ident, identb):
                pool.affine_select(out=m[:, :], in_=m[:, :], compare_op=ALU.not_equal, fill=1.0, base=0,
                                   pattern=[[-1, P]], channel_multiplier=1).then_inc(consts, 1)
            for k in range(3):
                link(pool.affine_select(out=sel[:, :, :], in_=sel[:, :, :], compare_op=ALU.not_equal, fill=1.0,
                                        base=-k * E, pattern=[[-1, E], [0, P]], channel_multiplier=1))
            for e in range(E):
                link(pool.memset(desc[:, :, e:e + 1], float(E - e)))
            link(pool.memset(onesb[:, :], 1.0))
            for k in range(QT):
                link(pool.memset(pow2[:, k:k + 1], float(2 ** k)))
            pool.memset(half[:, :], -0.5).then_inc(consts, 1)

            def low_part(u):
                pool.wait_ge(wh_done, u + 1)
                pool.tensor_tensor(wl[:, u, :, :], wraw_u[:, u, :, :], wh[:, u, :, :].bitcast(F32), ALU.subtract)\
                    .then_inc(wl_done, 1)

            for u in range(NU):
                low_part(u)
            pool.wait_ge(oc_mv, 1)
            link(pool.tensor_scalar(rstd[:, 0:1], mv[:, 0, 1:2], EPS, None, ALU.add))
            pool.tensor_tensor(rstd[:, 0:1], rstd[:, 0:1], half[:, 0:1], ALU.pow).then_inc(oc_rstd, 1)

            def after(b):
                wait_apart(pool, mv_done, (b + 1) * QT)
                pool.tensor_scalar(rstd[:, :], mv[:, :, 1], EPS, None, ALU.add).then_inc(ln_eps, 1)
                pool.wait_ge(ln_eps, b + 1)
                pool.tensor_tensor(rstd[:, :], rstd[:, :], half[:, :], ALU.pow).then_inc(rstd_done, 1)
                pool.wait_ge(oc_done, 1)
                pool.wait_ge(ob_out, 1 + b * 16)
                pool.tensor_tensor(obuf[:, :, :], xtok[:, bass.ds(b * QT, QT), :],
                                   oc[:, :].unsqueeze(1).to_broadcast([P, QT, H]), ALU.add).then_inc(ob_ready, 1)

            with pool.Fori(0, NB) as b:
                after(b)

            pool.wait_ge(wqh_done, 2)
            pool.tensor_tensor(wql[:, :, :], wq_raw, wqh[:, :, :].bitcast(F32), ALU.subtract).then_inc(wql_done, 1)
            pool.tensor_tensor(wkvl[:, :, :], wkv_raw, wkvh[:, :, :].bitcast(F32), ALU.subtract).then_inc(wql_done, 1)

            pool.wait_ge(down_done, CREDIT + TOT)
            pool.memset(kz[:, :, :, :], 0.0).then_inc(tiles_set, 1)
            pool.memset(v1[:, :, DH:D1], 1.0).then_inc(tiles_set, 1)
            pool.wait_ge(live_done, 1)
            live = pool.value_load(livei[0:1, 0:1], min_val=0, max_val=2 ** QT - 1)
            jobs = pool.alloc_register("pool_jobs")
            tiles = pool.alloc_register("pool_tiles")
            pool.reg_mov(jobs, 0)
            pool.reg_mov(tiles, 0)
            with pool.Fori(0, QT) as q:
                with pool.If((live & ((2 << q) - 1)) > 0):
                    t = pool.snap(tiles, min_val=0, max_val=QT)
                    wait_apart(pool, on_done, 1 + t * NB)
                    for b in range(NB):
                        ins = pool.tensor_copy(ost[:, b, :, :], nv1[:, :].unsqueeze(1).to_broadcast([P, NH, D1]))
                    ins.then_inc(o_init, 1)
                    with pool.Fori(0, q + 1) as k:
                        with pool.If(((live >> k) & 1) > 0):
                            j = pool.snap(jobs, min_val=0, max_val=QT * QT)
                            wait_apart(pool, bias_in, j * 16 + 16)
                            with pool.If(k < q):
                                pool.memset(nop1[:, :], 0.0).then_inc(bias_masked, 1)
                            with pool.If(k >= q):
                                pool.affine_select(out=bias, in_=bias, compare_op=ALU.is_ge, fill=-BIG, base=0,
                                                   pattern=[[0, NH], [-1, P]], channel_multiplier=1)\
                                    .then_inc(bias_masked, 1)
                            for b in range(NB):
                                pool.wait_ge(m_new, j * NB + b + 1)
                                for g in range(NG):
                                    hs = slice(g * HG, (g + 1) * HG)
                                    pool.tensor_tensor(ssb[:, b % 2, hs, :], ssb[:, b % 2, hs, :],
                                                       mstate[:, b, hs].unsqueeze(2).to_broadcast([P, HG, P]),
                                                       ALU.subtract).then_inc(s_shift, 1)
                                pool.wait_ge(alpha_done, 1 + j * NB + b + 1)
                                pool.wait_ge(o_added, 1 + (j * NB + b) * NG)
                                pool.wait_ge(o_init, t + 1)
                                pool.tensor_tensor(ost[:, b, :, :], ost[:, b, :, :],
                                                   alpha[:, b % 2, :].unsqueeze(2).to_broadcast([P, NH, D1]),
                                                   ALU.mult).then_inc(o_scaled, 1)
                            pool.reg_add(jobs, jobs, 1)
                    for b in range(NB):
                        wait_apart(pool, ln_mv, t * NB + b + 1)
                        pool.tensor_scalar(rstd[:, b:b + 1], mv[:, b, 1:2], EPS, None, ALU.add).then_inc(ln_eps, 1)
                        pool.wait_ge(ln_eps, NB + t * NB + b + 1)
                        pool.tensor_tensor(rstd[:, b:b + 1], rstd[:, b:b + 1], half[:, 0:1], ALU.pow)\
                            .then_inc(ln_rstd, 1)
                    pool.reg_add(tiles, tiles, 1)

        @block.scalar
        def _(act):
            act.dma_start(small[:, 0:H], wt).then_inc(small_in, 16)
            act.dma_start(small[:, H:H + G], wg).then_inc(small_in, 16)
            act.dma_start(small[0:NB, H + P:H + P + G], cond).then_inc(small_in, 16)
            act.dma_start(small[0:NB, H + P + G:H + P + 2 * G], cond).then_inc(small_in, 16)
            act.dma_start(masku[:, :], mask.rearrange("b s -> (b s)").unsqueeze(0)).then_inc(mask_in, 16)
            act.dma_start(gin[:, :], g_in.rearrange("(k p) -> p k", p=P),
                          allow_slow_non_contiguous=True).then_inc(vec_in, 16)
            act.dma_start(gout[:, :], g_out.partition_broadcast(P)).then_inc(vec_in, 16)
            act.dma_start(nbias[:, :], null_bias.partition_broadcast(P)).then_inc(vec_in, 16)
            act.dma_start(nv1[:, 0:DH], cond[1].partition_broadcast(P)).then_inc(vec_in, 16)
            act.sem_inc(g_free, CREDIT)
            act.sem_inc(y_free, CREDIT)

            def weight_high(u):
                act.wait_ge(w_in[UNIT_IN[u]], 16 * (5 if u < NSH else 6))
                act.activation(wh[:, u, :, :], wraw_u[:, u, :, :], ACT.Copy).then_inc(wh_done, 1)

            for b in range(NB):
                for k in range(KB):
                    act.wait_ge(xt_tr, KB * b + k + 1)
                    if b >= 2 and k == 0:
                        act.wait_ge(routed, b - 1)
                        act.wait_ge(xt_low, b - 1)
                    act.activation(xtf[:, b % 2, k, :], bank[2 * (b % 2) + k][:, :], ACT.Copy).then_inc(xt_ev, 1)
                if b == 0:
                    weight_high(0)
                    weight_high(1)
            act.wait_ge(dve_chain, CENTRED)
            act.activation(rt[1][:, :, :], rt[1][:, :, :], ACT.Exp, scale=0.5).then_inc(routed, 1)
            for u in range(NSH, NU):
                weight_high(u)

            def unit_high(b, s):
                n = b * NU + s
                act.wait_ge(u_free, n + 1 + CREDIT)
                act.wait_ge(down_done, n + 1)
                act.activation(huh[:, s % 2, :], hid[:, s % 2, :], ACT.Copy).then_inc(huh_done, 1)

            def xn_evac(b, k):
                act.wait_ge(m_ready, b * 4 + 3 + k)
                act.activation(yt[:, k, :], misc_ps[:, :], ACT.Copy, scale=gin[:, k:k + 1]).then_inc(m_free, 1)

            act.wait_ge(vec_in, 64)
            act.wait_ge(xt_low, NB)

            def experts(b, first):
                for s in range(NU):
                    if s >= 1:
                        unit_high(b, s - 1)
                    act.wait_ge(g_ready, b * NU + s + 1)
                    act.wait_ge(hul_done, b * NU + s + 1)
                    act.activation(hid[:, s % 2, :], gate_ps[s % 2][:, :], ACT.Copy).then_inc(g_free, 1)
                    if s in (6, 7) and not first:
                        xn_evac(b - 1, s - 6)
                unit_high(b, NU - 1)
                act.wait_ge(down_done, CREDIT + (b + 1) * NU)
                act.wait_ge(xnl_done, b * 2)
                for k in range(KB):
                    act.activation(yt[:, k, :], y_ps[k][:, :], ACT.Copy).then_inc(y_free, 1)

            experts(0, True)
            with act.Fori(1, NB) as b:
                experts(b, False)
            for k in range(KB):
                xn_evac(NB - 1, k)
            act.wait_ge(wq_in, 64)
            act.activation(wqh[:, :, :], wq_raw, ACT.Copy).then_inc(wqh_done, 1)
            act.activation(wkvh[:, :, :], wkv_raw, ACT.Copy).then_inc(wqh_done, 1)

            act.wait_ge(live_done, 1)
            live = act.value_load(livei[0:1, 0:1], min_val=0, max_val=2 ** QT - 1)
            jobs = act.alloc_register("act_jobs")
            tiles = act.alloc_register("act_tiles")
            act.reg_mov(jobs, 0)
            act.reg_mov(tiles, 0)
            with act.Fori(0, QT) as q:
                with act.If((live & ((2 << q) - 1)) > 0):
                    t = act.snap(tiles, min_val=0, max_val=QT)
                    for j in range(PAIRS):
                        act.wait_ge(q_ready, t * PAIRS + j + 1)
                        act.activation(qt_sb[:, j, :, :].rearrange("p b t -> p (b t)"), proj_ps[j % 2][:, :], ACT.Copy,
                                       scale=float(DH) ** -0.5).then_inc(q_evac, 1)
                    with act.Fori(0, q + 1) as k:
                        with act.If(((live >> k) & 1) > 0):
                            j = act.snap(jobs, min_val=0, max_val=QT * QT)
                            act.wait_ge(kv_ready, j + 1)
                            act.wait_ge(tiles_set, 2)
                            act.activation(kz[0:DH, :, 0, :], proj_ps[0][0:DH, :].rearrange("p (b t) -> p b t", b=NB),
                                           ACT.Copy).then_inc(kv_evac, 1)
                            act.activation(kz[DH:P, :, 1, :], proj_ps[0][DH:P, :].rearrange("p (b t) -> p b t", b=NB),
                                           ACT.Copy).then_inc(kv_evac, 1)
                            act.activation(vt[:, :, :].rearrange("p b t -> p (b t)"), proj_ps[1][0:DH, :],
                                           ACT.Copy).then_inc(kv_evac, 1)
                            act.wait_ge(v_ready, j + 1)
                            act.activation(v1[:, :, 0:DH], proj_ps[0][:, 0:NB * DH]
                                           .rearrange("p (b d) -> p b d", b=NB), ACT.Copy).then_inc(v_evac, 1)
                            for b in range(NB):
                                def probs(g):
                                    hs = slice(g * HG, (g + 1) * HG)
                                    act.wait_ge(s_shift, j * NW + b * NG + g + 1)
                                    act.activation(ssb[:, b % 2, hs, :], ssb[:, b % 2, hs, :], ACT.Exp)\
                                        .then_inc(p_done, 1)

                                def transposed(g):
                                    act.wait_ge(pt_ready, 1 + j * NW + b * NG + g + 1)
                                    act.activation(pt[:, g % 2, :, :].rearrange("p h t -> p (h t)"),
                                                   pt_ps[g % 2][:, :], ACT.Copy).then_inc(pt_evac, 1)

                                act.wait_ge(m_new, j * NB + b + 1)
                                act.activation(alpha[:, b % 2, :], dm[:, b % 2, :], ACT.Exp).then_inc(alpha_done, 1)
                                probs(0)
                                for g in range(1, NG):
                                    probs(g)
                                    transposed(g - 1)
                                transposed(NG - 1)
                            act.reg_add(jobs, jobs, 1)
                    for b in range(NB):
                        for i in range(2):
                            act.wait_ge(ot_ready, t * (2 * NB) + 2 * b + i + 1)
                            act.activation(ssb[:, 1, 8 * (b % 2) + 4 * i:8 * (b % 2) + 4 * i + 4, :]
                                           .rearrange("p h t -> p (h t)"), pt_ps[i][:, :], ACT.Copy)\
                                .then_inc(ot_evac, 1)
                    act.reg_add(tiles, tiles, 1)

        @block.vector
        def _(dve):
            chain = [0]

            def link(ins):
                chain[0] += 1
                ins.then_inc(dve_chain, 1)
                dve.wait_ge(dve_chain, chain[0])

            dve.sem_inc(u_free, CREDIT)
            dve.sem_inc(hul_done, CREDIT)
            dve.sem_inc(wb_free, 1)
            dve.wait_ge(small_tr, 1)
            link(dve.tensor_copy(wtT[:, :, :].rearrange("p k e -> p (k e)"), misc_ps[:, 0:KB * 8]))
            link(dve.tensor_copy(wgT[:, :], misc_ps[0:G, 16:24]))
            link(dve.tensor_copy(condT[:, :], misc_ps[:, 24:28]))
            for b in range(NB):
                link(dve.tensor_copy(gcol[:, b, :], condT[0:G, b:b + 1].to_broadcast([G, P])))
            link(dve.tensor_copy(nvc[:, :], condT[:, 1:2].to_broadcast([P, P])))
            link(dve.memset(nkz[:, :], 0.0))
            link(dve.tensor_copy(nkz[0:DH, 0:1], condT[0:DH, 0:1]))
            link(dve.tensor_copy(nkz[DH:P, 1:2], condT[DH:P, 0:1]))
            dve.memset(nv1[:, DH:D1], 1.0).then_inc(small_ev, 1)
            for b in range(NB):
                cols = slice(b * S, (b + 1) * S)
                dve.wait_ge(xt_ev, KB * (b + 1))
                dve.tensor_copy(xth[:, :, cols], xtf[:, b % 2, :, :]).then_inc(xt_high, 1)
                dve.wait_ge(xt_high, b + 1)
                dve.tensor_tensor(xtl[:, :, cols], xtf[:, b % 2, :, :], xth[:, :, cols].bitcast(F32),
                                  ALU.subtract).then_inc(xt_low, 1)

            full = [P, NT, E]
            e_, c_, k_, o_ = rt
            dve.wait_ge(routed, NB)
            link(dve.tensor_copy(c_[:, :, :].rearrange("p t e -> p (t e)"), wb_ps[:, 0:NT * E]))
            link(dve.reduce_max(r1[0][:, :, 0], c_[:, :, :], AX_X))
            link(dve.tensor_tensor(c_[:, :, :], c_[:, :, :], r1[0][:, :, :].to_broadcast(full), ALU.subtract))
            assert chain[0] == CENTRED, chain[0]
            dve.wait_ge(routed, NB + 1)
            link(dve.reduce_sum(r1[0][:, :, 0], c_[:, :, :], AX_X))
            link(dve.reciprocal(r1[0][:, :, :], r1[0][:, :, :]))
            link(dve.tensor_tensor(e_[:, :, :], c_[:, :, :], r1[0][:, :, :].to_broadcast(full), ALU.mult))
            dve.wait_ge(consts, 3)

            def best(src, hot, top):
                link(dve.reduce_max(top[:, :, 0], src[:, :, :], AX_X))
                link(dve.tensor_tensor(k_[:, :, :], src[:, :, :], top[:, :, :].to_broadcast(full), ALU.is_equal))
                link(dve.tensor_tensor(k_[:, :, :], k_[:, :, :], desc[:, :, :], ALU.mult))
                link(dve.reduce_max(r1[3][:, :, 0], k_[:, :, :], AX_X))
                link(dve.tensor_tensor(hot[:, :, :], k_[:, :, :], r1[3][:, :, :].to_broadcast(full), ALU.is_equal))

            best(e_, o_, r1[1])
            link(dve.scalar_tensor_tensor(out=c_[:, :, :], in0=o_[:, :, :], scalar=-2.0, in1=e_[:, :, :],
                                          op0=ALU.mult, op1=ALU.add))
            best(c_, c_, r1[2])
            link(dve.tensor_tensor(o_[:, :, :], o_[:, :, :], c_[:, :, :], ALU.add))
            link(dve.tensor_tensor(e_[:, :, :], e_[:, :, :], o_[:, :, :], ALU.mult))
            link(dve.tensor_tensor(r1[1][:, :, :], r1[1][:, :, :], r1[2][:, :, :], ALU.add))
            link(dve.tensor_scalar(r1[1][:, :, :], r1[1][:, :, :], 1e-20, None, ALU.add))
            link(dve.reciprocal(r1[1][:, :, :], r1[1][:, :, :]))
            link(dve.tensor_tensor(e_[:, :, :], e_[:, :, :], r1[1][:, :, :].to_broadcast(full), ALU.mult))
            link(dve.tensor_copy(w3[:, :, 0, :], e_[:, :, :]))
            link(dve.tensor_tensor(c_[:, :, :], e_[:, :, :], w3[:, :, 0, :], ALU.subtract))
            link(dve.tensor_copy(w3[:, :, 1, :], c_[:, :, :]))
            link(dve.tensor_tensor(e_[:, :, :], c_[:, :, :], w3[:, :, 1, :], ALU.subtract))
            dve.tensor_copy(w3[:, :, 2, :], e_[:, :, :]).then_inc(w3_ready, 1)
            dve.wait_ge(w3_tr, 1)
            dve.tensor_copy(w3t[:, 0:NT * P // 2], wb_ps[0:3 * E, :].bitcast(BF16)).then_inc(w3_ev, 1)
            dve.wait_ge(w3_tr, 2)
            dve.tensor_copy(w3t[:, NT * P // 2:NT * P], misc_ps[0:3 * E, :].bitcast(BF16)).then_inc(m_free, 1)

            dve.wait_ge(mask_in, 16)
            link(dve.tensor_scalar(maskb[:, :], masku[:, :], -1.0, BIG, ALU.add, ALU.mult))
            link(dve.tensor_reduce(live4[:, :], masku[:, :].rearrange("o (b k s) -> o k b s", b=NB, k=QT),
                                   AX_XY, ALU.max))
            link(dve.tensor_tensor(live4[:, :], live4[:, :], pow2[:, :], ALU.mult))
            link(dve.reduce_sum(livew[:, :], live4[:, :], AX_X))
            dve.tensor_copy(livei[:, :], livew[:, :]).then_inc(live_done, 1)

            def unit_low(b, s):
                dve.wait_ge(huh_done, b * NU + s + 1)
                dve.tensor_tensor(hul[:, s % 2, :], hid[:, s % 2, :], huh[:, s % 2, :].bitcast(F32), ALU.subtract)\
                    .then_inc(hul_done, 1)

            def null_row():
                dve.wait_ge(oc_ready, 1)
                dve.tensor_copy(oc[:, :], misc_ps[:, 0:H]).then_inc(m_free, 1)
                dve.wait_ge(m_free, 2)
                dve.bn_stats(st6[:, 0, :], oc[:, :]).then_inc(oc_stat, 1)
                dve.wait_ge(oc_stat, 1)
                dve.bn_aggr(mv[:, 0, :], st6[:, 0, :]).then_inc(oc_mv, 1)
                dve.wait_ge(oc_rstd, 1)
                dve.tensor_scalar(oc[:, :], oc[:, :], mv[:, 0, 0:1], rstd[:, 0:1], ALU.subtract, ALU.mult)\
                    .then_inc(oc_norm, 1)
                dve.wait_ge(oc_norm, 1)
                dve.wait_ge(vec_in, 64)
                dve.tensor_tensor(oc[:, :], oc[:, :], gout[:, :], ALU.mult).then_inc(oc_done, 1)

            def add_moe(b, i):
                dve.wait_ge(m_ready, b * 4 + 1 + i)
                rows = xtok[:, bass.ds(b * QT + 2 * i, 2), :]
                dve.tensor_tensor(rows, rows, misc_ps[:, :].rearrange("p (t h) -> p t h", t=2), ALU.add)\
                    .then_inc(m_free, 1)

            def stats(b):
                wait_apart(dve, m_free, OC_M + b * 4 + 2)
                for t in range(QT):
                    dve.bn_stats(st6[:, t, :], xtok[:, bass.ds(b * QT + t, 1), :]
                                 .rearrange("p a h -> p (a h)")).then_inc(st_done, 1)
                wait_apart(dve, st_done, (b + 1) * QT)
                for t in range(QT):
                    dve.bn_aggr(mv[:, t, :], st6[:, t, :]).then_inc(mv_done, 1)

            def normalise(b):
                dve.wait_ge(rstd_done, b + 1)
                for t in range(QT):
                    dve.tensor_scalar(xn[:, t, :], xtok[:, bass.ds(b * QT + t, 1), :].rearrange("p a h -> p (a h)"),
                                      mv[:, t, 0:1], rstd[:, t:t + 1], ALU.subtract, ALU.mult).then_inc(xn_done, 1)

            def split_xn(b, k):
                dve.wait_ge(m_free, OC_M + b * 4 + 3 + k)
                dst = xth[:, k, bass.ds(b * S, S)]
                dve.tensor_copy(dst, yt[:, k, :]).then_inc(xnh_done, 1)
                dve.wait_ge(xnh_done, b * 2 + k + 1)
                dve.tensor_tensor(xtl[:, k, bass.ds(b * S, S)], yt[:, k, :], dst.bitcast(F32), ALU.subtract)\
                    .then_inc(xnl_done, 1)

            def experts(b, first):
                for s in range(NU):
                    n = b * NU + s
                    if s >= 1:
                        unit_low(b, s - 1)
                    dve.wait_ge(g_free, n + 1 + CREDIT)
                    dve.scalar_tensor_tensor(out=hid[:, s % 2, :], in0=hid[:, s % 2, :], scalar=LEAK,
                                             in1=hid[:, s % 2, :], op0=ALU.mult, op1=ALU.max).then_inc(leaked, 1)
                    dve.wait_ge(leaked, n + 1)
                    if s >= NSH:
                        r = b * E + s - NSH
                        dve.wait_ge(wb_ready, r + 1)
                        dve.tensor_tensor(hid[:, s % 2, :], hid[:, s % 2, :], wb_ps[:, :], ALU.mult)\
                            .then_inc(wb_free, 1)
                        dve.wait_ge(wb_free, r + 2)
                    dve.wait_ge(u_ready, n + 1)
                    dve.tensor_tensor(hid[:, s % 2, :], hid[:, s % 2, :], up_ps[s % 2][:, :], ALU.mult)\
                        .then_inc(u_free, 1)
                    if first and s == NU - 1:
                        null_row()
                    if not first:
                        if s in (2, 3):
                            add_moe(b - 1, s - 2)
                        if s == 4:
                            stats(b - 1)
                        if s == 5:
                            normalise(b - 1)
                        if s in (6, 7):
                            split_xn(b - 1, s - 6)
                unit_low(b, NU - 1)

            experts(0, True)
            with dve.Fori(1, NB) as b:
                experts(b, False)
            for i in range(2):
                add_moe(NB - 1, i)
            stats(NB - 1)
            normalise(NB - 1)
            for k in range(KB):
                split_xn(NB - 1, k)

            dve.wait_ge(ob_out, 1 + 16 * NB)
            live = dve.value_load(livei[0:1, 0:1], min_val=0, max_val=2 ** QT - 1)
            jobs = dve.alloc_register("dve_jobs")
            tiles = dve.alloc_register("dve_tiles")
            dve.reg_mov(jobs, 0)
            dve.reg_mov(tiles, 0)
            with dve.Fori(0, QT) as q:
                with dve.If((live & ((2 << q) - 1)) > 0):
                    t = dve.snap(tiles, min_val=0, max_val=QT)
                    dve.wait_ge(null_ready, t + 1)
                    dve.tensor_tensor(mstate[:, :, :], proj_ps[0][:, 0:NB * NH].rearrange("p (b h) -> p b h", b=NB),
                                      nbias[:, :].unsqueeze(1).to_broadcast([P, NB, NH]), ALU.add).then_inc(m_init, 1)
                    with dve.Fori(0, q + 1) as k:
                        with dve.If(((live >> k) & 1) > 0):
                            j = dve.snap(jobs, min_val=0, max_val=QT * QT)

                            def gather(b):
                                for g in range(NG):
                                    dve.wait_ge(pv_ready, j * NW + b * NG + g + 1)
                                    if g == 0:
                                        dve.wait_ge(o_scaled, j * NB + b + 1)
                                    hs = slice(g * HG, (g + 1) * HG)
                                    dve.tensor_tensor(ost[:, b, hs, :], ost[:, b, hs, :],
                                                      pv_ps[g % 2][:, 0:HG * D1].rearrange("p (h d) -> p h d", h=HG),
                                                      ALU.add).then_inc(o_added, 1)

                            dve.wait_ge(bias_masked, j + 1)
                            for b in range(NB):
                                for g in range(NG):
                                    dve.wait_ge(s_ready, j * NW + b * NG + g + 1)
                                    if g == 0:
                                        if b >= 2:
                                            dve.wait_ge(pt_ready, 1 + j * NW + (b - 1) * NG)
                                        else:
                                            dve.wait_ge(pt_ready, 1 + j * NW)
                                            dve.wait_ge(wo_ready, 1 + t * NB)
                                    hs = slice(g * HG, (g + 1) * HG)
                                    dve.tensor_tensor(ssb[:, b % 2, hs, :],
                                                      logit_ps[g % 2][:, :].rearrange("p (h k) -> p h k", h=HG),
                                                      bias[:, hs, :], ALU.add).then_inc(s_added, 1)
                                dve.wait_ge(s_added, 1 + j * NW + (b + 1) * NG)
                                dve.reduce_max(mx[:, :], ssb[:, b % 2, :, :], AX_X).then_inc(s_max, 1)
                                dve.wait_ge(s_max, j * NB + b + 1)
                                dve.wait_ge(m_init, t + 1)
                                dve.tensor_tensor(mx[:, :], mx[:, :], mstate[:, b, :], ALU.max).then_inc(m_step, 1)
                                dve.wait_ge(m_step, j * NB + b + 1)
                                if b < 2:
                                    dve.wait_ge(alpha_done, 1 + j * NB)
                                else:
                                    dve.wait_ge(alpha_done, 1 + j * NB + b - 1)
                                dve.tensor_tensor(dm[:, b % 2, :], mstate[:, b, :], mx[:, :], ALU.subtract)\
                                    .then_inc(m_delta, 1)
                                dve.wait_ge(m_delta, j * NB + b + 1)
                                dve.tensor_copy(mstate[:, b, :], mx[:, :]).then_inc(m_new, 1)
                                if b >= 1:
                                    gather(b - 1)
                            gather(NB - 1)
                            dve.reg_add(jobs, jobs, 1)

                    j = dve.snap(jobs, min_val=0, max_val=QT * QT)
                    dve.wait_ge(o_added, 1 + j * NW)
                    for b in range(NB):
                        n = t * NB + b
                        if b == 0:
                            dve.wait_ge(on_done, 1 + n)
                        dve.reciprocal(rl[:, b, :], ost[:, b, :, DH]).then_inc(rl_done, 1)
                        dve.wait_ge(rl_done, n + 1)
                        if b >= 2:
                            dve.wait_ge(ot_ready, 2 * (n - 1))
                        else:
                            dve.wait_ge(pt_ready, 1 + j * NW)
                        dve.tensor_tensor(ssb[:, 0, 8 * (b % 2):8 * (b % 2) + 8, :]
                                          .rearrange("p a (c d) -> p (a c) d", d=DH),
                                          ost[:, b, :, 0:DH], rl[:, b, :].unsqueeze(2).to_broadcast([P, NH, DH]),
                                          ALU.mult).then_inc(on_done, 1)
                    for b in range(NB):
                        n = t * NB + b
                        acc = pv_ps[b % 2][:, 0:H]
                        dve.wait_ge(wo_ready, 1 + n + 1)
                        dve.bn_stats(st6[:, b, :], acc).then_inc(ln_stat, 1)
                        wait_apart(dve, ln_stat, n + 1)
                        dve.bn_aggr(mv[:, b, :], st6[:, b, :]).then_inc(ln_mv, 1)
                        dve.wait_ge(ln_rstd, n + 1)
                        if b == 0:
                            dve.wait_ge(row_out, 1 + t * (16 * NB))
                        dve.tensor_scalar(obuf[:, b, :], acc, mv[:, b, 0:1], rstd[:, b:b + 1],
                                          ALU.subtract, ALU.mult).then_inc(ln_norm, 1)
                        dve.wait_ge(ln_norm, 1 + n + 1)
                        dve.tensor_tensor(obuf[:, b, :], obuf[:, b, :], gout[:, :], ALU.mult).then_inc(ln_scale, 1)
                        dve.wait_ge(ln_scale, n + 1)
                        dve.tensor_tensor(obuf[:, b, :], obuf[:, b, :],
                                          xtok[:, bass.ds(b * QT + q, 1), :].rearrange("p a h -> p (a h)"),
                                          ALU.add).then_inc(row_done, 1)
                    dve.reg_add(tiles, tiles, 1)

        @block.tensor
        def _(pe):
            mm = nc.tensor.matmul
            tr = nc.tensor.transpose
            pe.sem_inc(down_done, CREDIT)
            pe.wait_ge(consts, 2)
            pe.wait_ge(small_in, 64)
            for k in range(KB):
                tr(misc_ps[:, 8 * k:8 * k + 8], small[:, k * P:(k + 1) * P], ident[0:8, 0:8])
            tr(misc_ps[0:G, 16:24], small[:, H:H + G], ident[0:8, 0:8])
            tr(misc_ps[:, 24:28], small[0:NB, H + P:H + 2 * P], ident[0:NB, 0:NB]).then_inc(small_tr, 1)
            for b in range(NB):
                pe.wait_ge(x_in[b], 16)
                for k in range(KB):
                    if b >= 2:
                        pe.wait_ge(xt_ev, KB * (b - 2) + k + 1)
                    for t in range(QT):
                        ins = tr(bank[2 * (b % 2) + k][:, t * P:(t + 1) * P],
                                 xtok[:, b * QT + t, k * P:(k + 1) * P], ident[:, :])
                    ins.then_inc(xt_tr, 1)
                if b == 0:
                    pe.wait_ge(small_ev, 1)
                pe.wait_ge(xt_ev, KB * (b + 1))
                for t in range(QT):
                    acc = wb_ps[:, (b * QT + t) * E:(b * QT + t + 1) * E]
                    for k in range(KB):
                        mm(acc, xtf[:, b % 2, k, t * P:(t + 1) * P], wtT[:, k, :], start=(k == 0), stop=False)
                    ins = mm(acc, gcol[:, b, :], wgT[:, :], start=False, stop=True)
                ins.then_inc(routed, 1)
            pe.wait_ge(w3_ready, 1)
            for i, dst in enumerate((wb_ps, misc_ps)):
                view = dst[0:3 * E, :].bitcast(BF16)
                for t in range(NT // 2):
                    ins = tr(view[:, t * P:(t + 1) * P],
                             w3[:, i * NT // 2 + t, :, :].rearrange("p k e -> p (k e)"), identb[:, :])
                ins.then_inc(w3_tr, 1)
            pe.wait_ge(w3_ev, 1)
            pe.wait_ge(m_free, 1)
            pe.wait_ge(xt_low, NB)

            def down(b, s):
                n = b * NU + s
                pe.wait_ge(hul_done, n + 1 + CREDIT)
                if s == 0:
                    pe.wait_ge(y_free, CREDIT + b * KB)
                for k in range(KB):
                    cols = slice(k * P, (k + 1) * P)
                    ins = split3(mm, y_ps[k][:, :], wh[:, s, 2, cols], wl[:, s, 2, cols],
                                 huh[:, s % 2, :], hul[:, s % 2, :], s == 0, s == NU - 1)
                ins.then_inc(down_done, 1)

            def null_row():
                pe.wait_ge(wo_in, 16)
                pe.wait_ge(m_free, 1)
                for j in range(PAIRS):
                    ins = mm(misc_ps[:, 0:H], nvc[:, :], wo[:, j, :], start=(j == 0), stop=(j == PAIRS - 1))
                ins.then_inc(oc_ready, 1)

            def moe_rows(b, i):
                pe.wait_ge(y_free, CREDIT + (b + 1) * KB)
                pe.wait_ge(m_free, OC_M + b * 4 + i)
                for t in range(2):
                    for k in range(KB):
                        ins = tr(misc_ps[:, t * H + k * P:t * H + (k + 1) * P],
                                 yt[:, k, (2 * i + t) * P:(2 * i + t + 1) * P], ident[:, :])
                ins.then_inc(m_ready, 1)

            def xn_cols(b, k):
                pe.wait_ge(xn_done, (b + 1) * QT)
                pe.wait_ge(m_free, OC_M + b * 4 + 2 + k)
                for t in range(QT):
                    ins = tr(misc_ps[:, t * P:(t + 1) * P], xn[:, t, k * P:(k + 1) * P], ident[:, :])
                ins.then_inc(m_ready, 1)

            def experts(b, first):
                for s in range(NU):
                    n = b * NU + s

                    def product(acc, kind):
                        for k in range(KB):
                            cols = slice(k * M, (k + 1) * M)
                            ins = split3(mm, acc, wh[:, s, kind, cols], wl[:, s, kind, cols],
                                         xth[:, k, bass.ds(b * S, S)], xtl[:, k, bass.ds(b * S, S)],
                                         k == 0, k == KB - 1)
                        return ins

                    pe.wait_ge(wl_done, s + 1)
                    pe.wait_ge(g_free, n + 1)
                    product(gate_ps[s % 2][:, :], 0).then_inc(g_ready, 1)
                    if s >= NSH:
                        wait_apart(pe, wb_free, b * E + s - NSH + 1)
                        mm(wb_ps[:, :], sel[:, s - NSH, :], w3t[:, bass.ds(b * S, S)], start=True, stop=True)\
                            .then_inc(wb_ready, 1)
                    pe.wait_ge(u_free, n + 1)
                    product(up_ps[s % 2][:, :], 1).then_inc(u_ready, 1)
                    if s >= 1:
                        down(b, s - 1)
                    if first and s == NU - 1:
                        null_row()
                    if not first:
                        if s in (2, 3):
                            moe_rows(b - 1, s - 2)
                        if s in (6, 7):
                            xn_cols(b - 1, s - 6)
                down(b, NU - 1)

            experts(0, True)
            with pe.Fori(1, NB) as b:
                experts(b, False)
            for i in range(2):
                moe_rows(NB - 1, i)
            for k in range(KB):
                xn_cols(NB - 1, k)

            pe.wait_ge(wql_done, 2)
            pe.wait_ge(xnl_done, 2 * NB)
            pe.wait_ge(m_free, OC_M + 4 * NB)
            pe.wait_ge(wb_free, 1 + NB * E)
            pe.wait_ge(live_done, 1)
            live = pe.value_load(livei[0:1, 0:1], min_val=0, max_val=2 ** QT - 1)
            jobs = pe.alloc_register("pe_jobs")
            tiles = pe.alloc_register("pe_tiles")
            pe.reg_mov(jobs, 0)
            pe.reg_mov(tiles, 0)

            def project(acc, high, low, tile):
                for k in range(KB):
                    ins = split3(mm, acc, high(k), low(k), xth_q[:, k, :, bass.ds(tile * P, P)],
                                 xtl_q[:, k, :, bass.ds(tile * P, P)], k == 0, k == KB - 1)
                return ins

            with pe.Fori(0, QT) as q:
                with pe.If((live & ((2 << q) - 1)) > 0):
                    t = pe.snap(tiles, min_val=0, max_val=QT)
                    for j in range(PAIRS):
                        if j >= 2:
                            pe.wait_ge(q_evac, t * PAIRS + j - 1)
                        project(proj_ps[j % 2][:, :], lambda k: wqh[:, k, j * P:(j + 1) * P],
                                lambda k: wql[:, k, j * P:(j + 1) * P], q).then_inc(q_ready, 1)
                    pe.wait_ge(q_evac, (t + 1) * PAIRS)
                    for b in range(NB):
                        for j in range(PAIRS):
                            ins = mm(proj_ps[0][:, b * NH + 2 * j:b * NH + 2 * j + 2], qt_sb[:, j, b, :], nkz[:, :],
                                     start=True, stop=True)
                    ins.then_inc(null_ready, 1)
                    with pe.Fori(0, q + 1) as k:
                        with pe.If(((live >> k) & 1) > 0):
                            j = pe.snap(jobs, min_val=0, max_val=QT * QT)
                            pe.wait_ge(m_init, t + 1)
                            pe.wait_ge(v_evac, 1 + j)
                            project(proj_ps[0][:, :], lambda kk: wkvh[:, kk, DH:3 * DH],
                                    lambda kk: wkvl[:, kk, DH:3 * DH], k)
                            ins = project(proj_ps[1][:, :], lambda kk: wkvh[:, kk, 0:2 * DH],
                                          lambda kk: wkvl[:, kk, 0:2 * DH], k)
                            ins.then_inc(kv_ready, 1)
                            wait_apart(pe, kv_evac, j * 3 + 3)
                            for b in range(NB):
                                ins = tr(proj_ps[0][:, b * DH:(b + 1) * DH], vt[:, b, :], ident[0:DH, 0:DH])
                            ins.then_inc(v_ready, 1)

                            def logits(b, g):
                                w = j * NW + b * NG + g
                                acc = logit_ps[g % 2]
                                wait_apart(pe, s_added, 1 + (w - 1 if b * NG + g >= 2 else j * NW))
                                mm(acc[:, :].rearrange("p (h k) -> p h k", h=HG), onesb[:, :],
                                   mask_q[:, b:b + 1, bass.ds(k * P, P)].to_broadcast([1, HG, P]),
                                   start=True, stop=False)
                                for i in range(2):
                                    ins = mm(acc[:, i * 2 * P:(i + 1) * 2 * P], qt_sb[:, 2 * g + i, b, :],
                                             kz[:, b, :, :].rearrange("p a k -> p (a k)"),
                                             start=False, stop=(i == 1))
                                ins.then_inc(s_ready, 1)

                            def transposes(b, g):
                                w = b * NG + g
                                pe.wait_ge(p_done, j * NW + w + 1)
                                pe.wait_ge(pt_evac, 1 + j * NW + max(w - 1, 0))
                                for i in range(HG):
                                    ins = tr(pt_ps[g % 2][:, i * P:(i + 1) * P], ssb[:, b % 2, g * HG + i, :],
                                             ident[:, :])
                                ins.then_inc(pt_ready, 1)

                            def values(b, g):
                                w = b * NG + g
                                pe.wait_ge(pt_evac, 1 + j * NW + w + 1)
                                pe.wait_ge(o_added, 1 + j * NW + max(w - 1, 0))
                                for i in range(HG):
                                    ins = mm(pv_ps[g % 2][:, i * D1:(i + 1) * D1], pt[:, g % 2, i, :], v1[:, b, :],
                                             start=True, stop=True)
                                ins.then_inc(pv_ready, 1)

                            def weighted(b):
                                transposes(b, 0)
                                for g in range(1, NG):
                                    transposes(b, g)
                                    values(b, g - 1)
                                values(b, NG - 1)

                            pe.wait_ge(ln_norm, 1 + t * NB)
                            for b in range(NB):
                                for g in range(NG):
                                    logits(b, g)
                                if b == 0:
                                    pe.wait_ge(v_evac, 1 + j + 1)
                                if b >= 1:
                                    weighted(b - 1)
                            weighted(NB - 1)
                            pe.reg_add(jobs, jobs, 1)

                    j = pe.snap(jobs, min_val=0, max_val=QT * QT)
                    pe.wait_ge(pt_evac, 1 + j * NW)
                    pe.wait_ge(o_added, 1 + j * NW)

                    def out_transposes(b):
                        n = t * NB + b
                        pe.wait_ge(on_done, 1 + n + 1)
                        for i in range(2):
                            if b >= 1:
                                pe.wait_ge(ot_evac, 2 * (n - 1) + i + 1)
                            for c in range(4):
                                ins = tr(pt_ps[i][:, c * P:(c + 1) * P], ssb[:, 0, 8 * (b % 2) + 4 * i + c, :],
                                         ident[:, :])
                            ins.then_inc(ot_ready, 1)

                    def out_project(b):
                        n = t * NB + b
                        pe.wait_ge(ot_evac, 2 * (n + 1))
                        if b >= 2:
                            pe.wait_ge(ln_norm, 1 + n - 1)
                        for jj in range(PAIRS):
                            ins = mm(pv_ps[b % 2][:, 0:H], ssb[:, 1, 8 * (b % 2) + jj, :], wo[:, jj, :],
                                     start=(jj == 0), stop=(jj == PAIRS - 1))
                        ins.then_inc(wo_ready, 1)

                    for b in range(NB):
                        out_transposes(b)
                        out_project(b)
                    pe.reg_add(tiles, tiles, 1)


CENTRED = 14


_INS = ["x", "cond_64", "fside_16xSxS_0", "mask_BxS_bk0", "L0_cond_wt", "L0_cond_wg", "L0_cond_w_gate",
        "L0_cond_w_up", "L0_cond_w_down", "L0_cond_sw_gate", "L0_cond_sw_up", "L0_cond_sw_down", "L1_cond_g_in",
        "L1_cond_null_attn_bias", "L1_cond_Wq", "L1_cond_Wkv", "L1_cond_Wo", "L1_cond_g_out"]


def kernel(**inputs):
    import numpy as _np
    import concourse.bacc as _bacc
    from concourse import mybir as _mybir
    from concourse.bass_utils import run_bass_kernel_spmd as _run

    nc = _bacc.Bacc("TRN2", target_bir_lowering=False, num_devices=1)
    arrays, args = {}, []
    for name in _INS:
        a = _np.ascontiguousarray(inputs[name])
        arrays[f"in_{name}"] = a
        args.append(nc.dram_tensor(f"in_{name}", a.shape, _mybir.dt.from_np(a.dtype), kind="ExternalInput").ap())
    shape = inputs["x"].shape
    args.append(nc.dram_tensor("out_x", shape, _mybir.dt.float32, kind="ExternalOutput").ap())
    moe_then_attention(nc, *args)
    r = _run(nc, [arrays], core_ids=[0])
    return r.results[0]["out_x"]
```

```python
from contextlib import ExitStack

import concourse.bass as bass
from concourse import mybir

P = 128
F32 = mybir.dt.float32
F32R = mybir.dt.float32r
BF16 = mybir.dt.bfloat16
U8 = mybir.dt.uint8
I32 = mybir.dt.int32
ALU = mybir.AluOpType
ACT = mybir.ActivationFunctionType
AX_X = mybir.AxisListType.X
AX_XY = mybir.AxisListType.XY

BIG = 1e30
EPS = 1e-5
LEAK = 0.01
CREDIT = 2


def moe_then_attention(nc, x, cond, fside, mask, wt, wg, w_gate, w_up, w_down, sw_gate, sw_up, sw_down,
                       g_in, null_bias, w_q, w_kv, w_o, g_out, out):
    NB, S, H = x.shape
    E = w_gate.shape[0]
    M = w_gate.shape[2]
    NSH = sw_gate.shape[1] // M
    NU = NSH + E
    G = cond.shape[1]
    NH = fside.shape[0]
    INNER = w_q.shape[1]
    DH = INNER // NH
    KB = H // P
    QT = S // P
    NT = NB * QT
    NC = QT
    PAIRS = NH // 2
    HG = 4
    NG = NH // HG
    D1 = DH + 1
    NW = NB * NG
    assert M == P and S == 512 and KB == 2 and DH == 64 and NB == QT == 4 and NSH == 2 and NU % 2 == 0 and G == DH

    with ExitStack() as ctx:
        def sb(name, shape, dt=F32):
            return ctx.enter_context(nc.sbuf_tensor(name, shape, dt))

        def sem(name):
            return ctx.enter_context(nc.semaphore(name))

        bank = [ctx.enter_context(nc.psum_tensor(f"bank{i}", [P, 512], F32)) for i in range(8)]
        gate_ps, up_ps, wb_ps, y_ps, misc_ps = bank[0:2], bank[2:4], bank[4], bank[5:7], bank[7]
        logit_ps, pt_ps, pv_ps, proj_ps = bank[0:2], bank[2:4], bank[5:7], (bank[4], bank[7])
        s_ps = (*logit_ps, *proj_ps)

        xtok = sb("xtok", [P, NT, H])
        xtf = sb("xtf", [P, 2, KB, S])
        xth = sb("xth", [P, KB, NB * S], F32R)
        xtl = sb("xtl", [P, KB, NB * S], F32R)
        wraw = sb("wraw", [P, NU * 3 * 256])
        wqh = sb("wqh", [P, KB, INNER], F32R)
        wql = sb("wql", [P, KB, INNER], F32R)
        wkvh = sb("wkvh", [P, KB, 3 * DH], F32R)
        wkvl = sb("wkvl", [P, KB, 3 * DH], F32R)
        wo = sb("wo", [P, PAIRS, H])
        hid = sb("hid", [P, 2, S])
        huh = sb("huh", [P, 2, S], F32R)
        hul = sb("hul", [P, 2, S], F32R)
        obuf = sb("obuf", [P, QT, H])
        ident = sb("ident", [P, P])
        identb = sb("identb", [P, P], BF16)
        small = hid[0:8, 1, :]
        wtT = sb("wtT", [P, KB, 8])
        wgT = sb("wgT", [G, 8])
        condT = sb("condT", [P, 4])
        gcol = hid[0:G, 0, :].rearrange("p (b t) -> p b t", b=NB)
        glog = sb("glog", [P, NB, E])
        nkb = sb("nkb", [P, DH])
        wnf = sb("wnf", [P, KB, NH])
        wnh = sb("wnh", [P, KB, NH], F32R)
        wnl = sb("wnl", [P, KB, NH], F32R)
        nvc = sb("nvc", [P, P])
        nv1 = sb("nv1", [P, D1])
        nbias = sb("nbias", [P, NH])
        gin = sb("gin", [P, KB])
        gout = sb("gout", [P, H])
        oc = sb("oc", [P, H])
        masku = obuf[0:1, 2:4, :].rearrange("p t h -> p (t h)").bitcast(U8)
        maskb = sb("maskb", [1, NB * S], BF16)
        onesb = sb("onesb", [1, P], BF16)
        live4 = sb("live4", [1, QT])
        pow2 = sb("pow2", [1, QT])
        livew = sb("livew", [1, 1])
        livei = sb("livei", [1, 1], I32)
        rt = [obuf[:, i // 2, (i % 2) * NT * E:(i % 2 + 1) * NT * E].rearrange("p (t e) -> p t e", e=E)
              for i in range(4)]
        r1 = [sb(f"r1{i}", [P, NT, 1]) for i in range(4)]
        desc = sb("desc", [P, NT, E])
        w3 = sb("w3", [P, NT, 3, E], BF16)
        w3t = sb("w3t", [3 * E, NT * P], BF16)
        sel = sb("sel", [3 * E, E, P], BF16)
        st6 = sb("st6", [P, QT, 6])
        mv = sb("mv", [P, QT, 2])
        rstd = sb("rstd", [P, QT])
        half = sb("half", [P, QT])
        mx = sb("mx", [P, NH])
        mneg = sb("mneg", [P, NB, NH])
        dm = sb("dm", [P, 2, NH])
        alpha = sb("alpha", [P, 2, NH])
        rl = sb("rl", [P, NB, NH])

        with ExitStack() as early:
            wh = early.enter_context(nc.sbuf_tensor("wh", [P, NU, 3, 256], F32R))
            wl = early.enter_context(nc.sbuf_tensor("wl", [P, NU, 3, 256], F32R))
        qt_sb = sb("qt_sb", [P, PAIRS, NB, P])
        ost = sb("ost", [P, NB, NH, D1])
        kz = sb("kz", [P, NB, 2, P])
        vt = sb("vt", [DH, NB, P])
        v1 = sb("v1", [P, NB, D1])
        ssb = sb("ssb", [P, 2, NH, P])
        pt = sb("pt", [P, 2, HG, P])

        null_t = ssb[0:NH, 1, 0:NB, :]
        wn_products = xtf[:, :, :, :].rearrange("p c k s -> p (c k s)").rearrange("p (n d) -> p n d", d=DH)
        yt = xtf[:, 0, :, :]
        xn = xtf[:, 1, :, :].rearrange("p k (t h) -> p (k t) h", h=H)
        wraw_u = wraw[:, :].rearrange("p (u w n) -> p u w n", u=NU, w=3)
        bias = wraw[:, 0:NH * P].rearrange("p (h k) -> p h k", h=NH)
        wq_raw = wraw[:, NH * P:NH * P + KB * INNER].rearrange("p (k n) -> p k n", k=KB)
        wkv_raw = wraw[:, NH * P + KB * INNER:NH * P + KB * INNER + KB * 3 * DH].rearrange("p (k n) -> p k n", k=KB)
        mask_q = maskb[:, :].rearrange("o (b s) -> o b s", b=NB)
        out_t = out.rearrange("b (t p) h -> t p b h", p=P)
        x_t = x.rearrange("b (t p) h -> t p b h", p=P)

        x_in = [sem(f"x_in{b}") for b in range(NB)]
        small_in = sem("small_in")
        w_in = [sem(f"w_in{i}") for i in range(1 + E // 2)]
        wq_in = sem("wq_in")
        wo_in = sem("wo_in")
        vec_in = sem("vec_in")
        mask_in = sem("mask_in")
        zeroed = sem("zeroed")
        consts = sem("consts")
        small_tr = sem("small_tr")
        small_ev = sem("small_ev")
        xt_tr = sem("xt_tr")
        xt_ev = sem("xt_ev")
        xt_high = sem("xt_high")
        xt_low = sem("xt_low")
        routed = sem("routed")
        dve_chain = sem("dve_chain")
        pool_chain = sem("pool_chain")
        w3_ready = sem("w3_ready")
        w3_tr = sem("w3_tr")
        w3_ev = sem("w3_ev")
        wh_done = sem("wh_done")
        wl_done = sem("wl_done")
        wqh_done = sem("wqh_done")
        wql_done = sem("wql_done")
        wn_multiplied = sem("wn_multiplied")
        wn_summed = sem("wn_summed")
        wn_done = sem("wn_done")
        live_done = sem("live_done")
        g_ready = sem("g_ready")
        g_free = sem("g_free")
        u_ready = sem("u_ready")
        u_free = sem("u_free")
        wb_ready = sem("wb_ready")
        wb_free = sem("wb_free")
        leaked = sem("leaked")
        huh_done = sem("huh_done")
        hul_done = sem("hul_done")
        down_done = sem("down_done")
        y_free = sem("y_free")
        m_ready = sem("m_ready")
        m_free = sem("m_free")
        oc_ready = sem("oc_ready")
        oc_stat = sem("oc_stat")
        oc_mv = sem("oc_mv")
        oc_rstd = sem("oc_rstd")
        oc_norm = sem("oc_norm")
        oc_done = sem("oc_done")
        st_done = sem("st_done")
        mv_done = sem("mv_done")
        rstd_done = sem("rstd_done")
        xn_done = sem("xn_done")
        xnh_done = sem("xnh_done")
        xnl_done = sem("xnl_done")
        ob_ready = sem("ob_ready")
        ob_out = sem("ob_out")
        tiles_set = sem("tiles_set")
        q_ready = sem("q_ready")
        q_evac = sem("q_evac")
        null_ready = sem("null_ready")
        null_evac = sem("null_evac")
        null_tr = sem("null_tr")
        m_init = sem("m_init")
        o_init = sem("o_init")
        bias_in = sem("bias_in")
        bias_masked = sem("bias_masked")
        kv_ready = sem("kv_ready")
        kv_evac = sem("kv_evac")
        v_ready = sem("v_ready")
        v_evac = sem("v_evac")
        s_ready = sem("s_ready")
        s_added = sem("s_added")
        s_max = sem("s_max")
        m_delta = sem("m_delta")
        m_new = sem("m_new")
        m_step = sem("m_step")
        alpha_done = sem("alpha_done")
        p_done = sem("p_done")
        pt_ready = sem("pt_ready")
        pt_evac = sem("pt_evac")
        pv_ready = sem("pv_ready")
        o_scaled = sem("o_scaled")
        o_added = sem("o_added")
        rl_done = sem("rl_done")
        on_done = sem("on_done")
        ot_ready = sem("ot_ready")
        ot_evac = sem("ot_evac")
        wo_ready = sem("wo_ready")
        ln_stat = sem("ln_stat")
        ln_mv = sem("ln_mv")
        ln_rstd = sem("ln_rstd")
        ln_eps = sem("ln_eps")
        ln_norm = sem("ln_norm")
        ln_scale = sem("ln_scale")
        row_done = sem("row_done")
        row_out = sem("row_out")
        passed = sem("passed")

        block = ctx.enter_context(nc.Block())

        UNIT_IN = [0] * NSH + [1 + e // 2 for e in range(E)]
        def tile_of(c):
            return (c + QT - 1) & (QT - 1)

        def chunk_of(tile):
            return (tile + 1) & (QT - 1)

        OC_M = 2
        TOT = NB * NU

        primed = (s_added, pt_ready, wo_ready, alpha_done, o_added, on_done, ln_norm, v_evac, pt_evac, row_out,
                  ob_out)

        def wait_apart(eng, semaphore, value):
            eng.wait_ge(semaphore, value)
            eng.sem_inc(passed, 1)

        def split3(mm, acc, wa, wb_, ra, rb, first, last):
            mm(acc, wa, ra, start=first, stop=False)
            mm(acc, wa, rb, start=False, stop=False)
            return mm(acc, wb_, ra, start=False, stop=last)

        @block.sync
        def _(sp):
            for semaphore in primed:
                sp.sem_inc(semaphore, 1)
            for c in range(NC):
                sp.dma_start(xtok[:, c * NB:(c + 1) * NB, :], x_t[tile_of(c)]).then_inc(x_in[c], 16)
            for kind, src in ((0, sw_gate), (1, sw_up)):
                for u in range(NSH):
                    sp.dma_start(wraw_u[:, u, kind, :].rearrange("p (k m) -> p k m", k=KB),
                                 src.rearrange("(k p) (u m) -> u p k m", p=P, u=NSH)[u]).then_inc(w_in[0], 16)
            sp.dma_start(wraw_u[:, 0:NSH, 2, :], sw_down.rearrange("(u p) h -> p u h", p=P)).then_inc(w_in[0], 16)
            for i in range(E // 2):
                for e in (2 * i, 2 * i + 1):
                    for kind, src in ((0, w_gate), (1, w_up)):
                        sp.dma_start(wraw_u[:, NSH + e, kind, :].rearrange("p (k m) -> p k m", k=KB),
                                     src[e].rearrange("(k p) m -> p k m", p=P)).then_inc(w_in[1 + i], 16)
                    sp.dma_start(wraw_u[:, NSH + e, 2, :], w_down[e]).then_inc(w_in[1 + i], 16)
            sp.dma_start(wo[:, :, :], w_o.rearrange("(j p) h -> p j h", p=P)).then_inc(wo_in, 16)
            sp.wait_ge(wh_done, NU)
            sp.wait_ge(wl_done, NU)
            sp.dma_start(wq_raw, w_q.rearrange("(k p) n -> p k n", p=P)).then_inc(wq_in, 16)
            kvr = w_kv.rearrange("(k p) n -> p k n", p=P)
            sp.dma_start(wkv_raw[:, :, 0:DH], kvr[:, :, DH:2 * DH]).then_inc(wq_in, 16)
            sp.dma_start(wkv_raw[:, :, DH:2 * DH], kvr[:, :, 0:DH]).then_inc(wq_in, 16)
            sp.dma_start(wkv_raw[:, :, 2 * DH:3 * DH], kvr[:, :, 0:DH]).then_inc(wq_in, 16)

            sp.wait_ge(live_done, 1)
            live = sp.value_load(livei[0:1, 0:1], min_val=0, max_val=2 ** QT - 1)
            jobs = sp.alloc_register("sp_jobs")
            sp.reg_mov(jobs, 0)
            with sp.Fori(0, QT) as t:
                q = (QT - 1) - t
                with sp.If((live & ((2 << q) - 1)) > 0):
                    with sp.Fori(0, q + 1) as back:
                        k = (q - back).with_bounds(min_val=0, max_val=QT - 1)
                        with sp.If(((live >> k) & 1) > 0):
                            j = sp.snap(jobs, min_val=0, max_val=QT * QT)
                            sp.wait_ge(s_added, 1 + j * NW)
                            sp.dma_start(bias, fside[:, bass.ds(q * P, P), bass.ds(k * P, P)]
                                         .rearrange("h p k -> p h k")).then_inc(bias_in, 16)
                            sp.reg_add(jobs, jobs, 1)
                    sp.wait_ge(ob_out, 1 + 16 * NC)
                    for b in range(NB):
                        sp.wait_ge(row_done, t * NB + b + 1)
                        sp.dma_start(out_t[bass.ds(q, 1), :, b, :].rearrange("a p h -> p a h"),
                                     obuf[:, b:b + 1, :]).then_inc(row_out, 16)
                    wait_apart(sp, row_out, 1 + t * (16 * NB) + 16 * NB)
            sp.wait_ge(ob_out, 1 + 16 * NC)

        @block.gpsimd
        def _(pool):
            def link(ins, n=[0]):
                n[0] += 1
                ins.then_inc(pool_chain, 1)
                pool.wait_ge(pool_chain, n[0])

            pool.memset(ident[:, :], 0.0).then_inc(zeroed, 1)
            pool.memset(identb[:, :], 0.0).then_inc(zeroed, 1)
            pool.memset(sel[:, :, :], 0.0).then_inc(zeroed, 1)
            pool.wait_ge(zeroed, 3)
            for m in (ident, identb):
                pool.affine_select(out=m[:, :], in_=m[:, :], compare_op=ALU.not_equal, fill=1.0, base=0,
                                   pattern=[[-1, P]], channel_multiplier=1).then_inc(consts, 1)
            for k in range(3):
                link(pool.affine_select(out=sel[:, :, :], in_=sel[:, :, :], compare_op=ALU.not_equal, fill=1.0,
                                        base=-k * E, pattern=[[-1, E], [0, P]], channel_multiplier=1))
            for e in range(E):
                link(pool.memset(desc[:, :, e:e + 1], float(E - e)))
            link(pool.memset(onesb[:, :], 1.0))
            for k in range(QT):
                link(pool.memset(pow2[:, k:k + 1], float(2 ** k)))
            pool.memset(half[:, :], -0.5).then_inc(consts, 1)

            def low_part(u):
                pool.wait_ge(wh_done, u + 1)
                pool.tensor_tensor(wl[:, u, :, :], wraw_u[:, u, :, :], wh[:, u, :, :].bitcast(F32), ALU.subtract)\
                    .then_inc(wl_done, 1)

            for u in range(NU):
                low_part(u)
            pool.wait_ge(vec_in, 80)
            pool.wait_ge(wq_in, 64)
            pool.wait_ge(xt_low, NC)
            pool.wait_ge(routed, NC)
            pool.tensor_tensor(wn_products, wq_raw.rearrange("p k (h d) -> p (k h) d", d=DH),
                               nkb[:, :].unsqueeze(1).to_broadcast([P, KB * NH, DH]), ALU.mult)\
                .then_inc(wn_multiplied, 1)
            pool.wait_ge(wqh_done, 2)
            pool.tensor_tensor(wql[:, :, :], wq_raw, wqh[:, :, :].bitcast(F32), ALU.subtract).then_inc(wql_done, 1)
            pool.tensor_tensor(wkvl[:, :, :], wkv_raw, wkvh[:, :, :].bitcast(F32), ALU.subtract).then_inc(wql_done, 1)

            def after(b):
                wait_apart(pool, mv_done, (b + 1) * QT)
                pool.tensor_scalar(rstd[:, :], mv[:, :, 1], EPS, None, ALU.add).then_inc(ln_eps, 1)
                pool.wait_ge(ln_eps, b + 1)
                pool.tensor_tensor(rstd[:, :], rstd[:, :], half[:, :], ALU.pow).then_inc(rstd_done, 1)
                pool.wait_ge(oc_done, 1)
                pool.wait_ge(ob_out, 1 + b * 16)
                pool.tensor_tensor(obuf[:, :, :], xtok[:, bass.ds(b * QT, QT), :],
                                   oc[:, :].unsqueeze(1).to_broadcast([P, QT, H]), ALU.add).then_inc(ob_ready, 1)

            pool.wait_ge(oc_mv, 1)
            link(pool.tensor_scalar(rstd[:, 0:1], mv[:, 0, 1:2], EPS, None, ALU.add))
            pool.tensor_tensor(rstd[:, 0:1], rstd[:, 0:1], half[:, 0:1], ALU.pow).then_inc(oc_rstd, 1)

            with pool.Fori(0, NC - 1) as c:
                after(c)
            pool.wait_ge(down_done, CREDIT + TOT)
            pool.memset(kz[:, :, :, :], 0.0).then_inc(tiles_set, 1)
            pool.memset(v1[:, :, DH:D1], 1.0).then_inc(tiles_set, 1)
            after(NC - 1)
            pool.wait_ge(live_done, 1)
            live = pool.value_load(livei[0:1, 0:1], min_val=0, max_val=2 ** QT - 1)
            jobs = pool.alloc_register("pool_jobs")
            pool.reg_mov(jobs, 0)
            with pool.Fori(0, QT) as t:
                q = (QT - 1) - t
                with pool.If((live & ((2 << q) - 1)) > 0):
                    with pool.Fori(0, q + 1) as back:
                        k = (q - back).with_bounds(min_val=0, max_val=QT - 1)
                        with pool.If(((live >> k) & 1) > 0):
                            j = pool.snap(jobs, min_val=0, max_val=QT * QT)
                            wait_apart(pool, bias_in, j * 16 + 16)
                            with pool.If(back > 0):
                                pool.sem_inc(bias_masked, 1)
                            with pool.If(back < 1):
                                pool.affine_select(out=bias, in_=bias, compare_op=ALU.is_ge, fill=-BIG, base=0,
                                                   pattern=[[0, NH], [-1, P]], channel_multiplier=1)\
                                    .then_inc(bias_masked, 1)
                            for b in range(NB):
                                pool.wait_ge(alpha_done, 1 + j * NB + b + 1)
                                pool.wait_ge(o_added, 1 + (j * NB + b) * NG)
                                pool.wait_ge(o_init, (t + 1) * NB)
                                pool.tensor_tensor(ost[:, b, :, :], ost[:, b, :, :],
                                                   alpha[:, b % 2, :].unsqueeze(2).to_broadcast([P, NH, D1]),
                                                   ALU.mult).then_inc(o_scaled, 1)
                            pool.reg_add(jobs, jobs, 1)
                    for b in range(NB):
                        wait_apart(pool, ln_mv, t * NB + b + 1)
                        pool.tensor_scalar(rstd[:, b:b + 1], mv[:, b, 1:2], EPS, None, ALU.add).then_inc(ln_eps, 1)
                        pool.wait_ge(ln_eps, NB + t * NB + b + 1)
                        pool.tensor_tensor(rstd[:, b:b + 1], rstd[:, b:b + 1], half[:, 0:1], ALU.pow)\
                            .then_inc(ln_rstd, 1)

        @block.scalar
        def _(act):
            act.dma_start(small[:, 0:H], wt).then_inc(small_in, 16)
            act.dma_start(small[:, H:H + G], wg).then_inc(small_in, 16)
            act.dma_start(small[0:NB, H + P:H + P + G], cond).then_inc(small_in, 16)
            act.dma_start(small[0:NB, H + P + G:H + P + 2 * G], cond).then_inc(small_in, 16)
            act.dma_start(masku[:, :], mask.rearrange("b s -> (b s)").unsqueeze(0)).then_inc(mask_in, 16)
            act.dma_start(gin[:, :], g_in.rearrange("(k p) -> p k", p=P),
                          allow_slow_non_contiguous=True).then_inc(vec_in, 16)
            act.dma_start(gout[:, :], g_out.partition_broadcast(P)).then_inc(vec_in, 16)
            act.dma_start(nbias[:, :], null_bias.partition_broadcast(P)).then_inc(vec_in, 16)
            act.dma_start(nv1[:, 0:DH], cond[1].partition_broadcast(P)).then_inc(vec_in, 16)
            act.dma_start(nkb[:, :], cond[0].partition_broadcast(P)).then_inc(vec_in, 16)
            act.sem_inc(g_free, CREDIT)
            act.sem_inc(y_free, CREDIT)

            def weight_high(u):
                act.wait_ge(w_in[UNIT_IN[u]], 16 * (5 if u < NSH else 6))
                act.activation(wh[:, u, :, :], wraw_u[:, u, :, :], ACT.Copy).then_inc(wh_done, 1)

            for c in range(NC):
                for k in range(KB):
                    act.wait_ge(xt_tr, KB * c + k + 1)
                    if c >= 2 and k == 0:
                        act.wait_ge(routed, c - 1)
                        act.wait_ge(xt_low, c - 1)
                    act.activation(xtf[:, c % 2, k, :], bank[2 * (c % 2) + k][:, :], ACT.Copy).then_inc(xt_ev, 1)
                weight_high(c)
            act.wait_ge(dve_chain, CENTRED)
            act.activation(rt[1][:, :, :], rt[1][:, :, :], ACT.Exp, scale=0.5).then_inc(routed, 1)

            def unit_high(b, s):
                n = b * NU + s
                act.wait_ge(u_free, n + 1 + CREDIT)
                act.wait_ge(down_done, n + 1)
                act.activation(huh[:, s % 2, :], hid[:, s % 2, :], ACT.Copy).then_inc(huh_done, 1)

            def xn_evac(b, k):
                act.wait_ge(m_ready, b * 4 + 3 + k)
                act.activation(yt[:, k, :], misc_ps[:, :], ACT.Copy, scale=gin[:, k:k + 1]).then_inc(m_free, 1)

            act.wait_ge(vec_in, 80)

            def sum_evac(b):
                act.wait_ge(down_done, CREDIT + (b + 1) * NU)
                act.wait_ge(xnl_done, b * 2)
                for k in range(KB):
                    act.activation(yt[:, k, :], y_ps[k][:, :], ACT.Copy).then_inc(y_free, 1)

            def store(b):
                act.wait_ge(ob_ready, b + 1)
                act.dma_start(out_t[bass.ds(tile_of(b), 1)].rearrange("a p b h -> p (a b) h"), obuf[:, :, :]).then_inc(ob_out, 16)

            def experts(b, first):
                for s in range(NU):
                    if s >= 1:
                        unit_high(b, s - 1)
                    elif not first:
                        unit_high(b - 1, NU - 1)
                    act.wait_ge(g_ready, b * NU + s + 1)
                    act.wait_ge(hul_done, b * NU + s + 1)
                    act.activation(hid[:, s % 2, :], gate_ps[s % 2][:, :], ACT.Copy).then_inc(g_free, 1)
                    if first and s + NC < NU:
                        weight_high(s + NC)
                    if first and s == NU - 2:
                        act.wait_ge(wq_in, 64)
                        act.activation(wqh[:, :, :], wq_raw, ACT.Copy).then_inc(wqh_done, 1)
                        act.activation(wkvh[:, :, :], wkv_raw, ACT.Copy).then_inc(wqh_done, 1)
                    if not first:
                        if s == 0:
                            act.wait_ge(wn_summed, 1)
                            sum_evac(b - 1)
                        if s in (6, 7):
                            xn_evac(b - 1, s - 6)
                        if s == 8:
                            store(b - 1)

            experts(0, True)
            with act.Fori(1, NC) as b:
                experts(b, False)
            unit_high(NC - 1, NU - 1)
            sum_evac(NC - 1)

            def null_evacuate(t):
                if not isinstance(t, int):
                    act.wait_ge(wo_ready, 1 + t * NB)
                act.wait_ge(null_ready, t + 1)
                act.activation(null_t, proj_ps[0][0:NH, :].rearrange("h (b t) -> h b t", b=NB), ACT.Copy,
                               scale=float(DH) ** -0.5).then_inc(null_evac, 1)

            def q_evacuate(t, j):
                act.wait_ge(q_ready, t * PAIRS + j + 1)
                act.activation(qt_sb[:, j, :, :].rearrange("p b t -> p (b t)"), logit_ps[j % 2][:, :], ACT.Copy,
                               scale=float(DH) ** -0.5).then_inc(q_evac, 1)

            def start_output(t, b):
                if b == 0 and not isinstance(t, int):
                    act.wait_ge(on_done, 1 + t * NB)
                act.activation(ost[:, b, :, :], nv1[:, :].unsqueeze(1).to_broadcast([P, NH, D1]), ACT.Copy)\
                    .then_inc(o_init, 1)

            null_evacuate(0)
            for j in range(PAIRS):
                if j == PAIRS - 1:
                    xn_evac(NC - 1, 0)
                q_evacuate(0, j)
                if 1 <= j < 1 + NB:
                    start_output(0, j - 1)
            xn_evac(NC - 1, 1)
            store(NC - 1)

            act.wait_ge(live_done, 1)
            live = act.value_load(livei[0:1, 0:1], min_val=0, max_val=2 ** QT - 1)
            jobs = act.alloc_register("act_jobs")
            act.reg_mov(jobs, 0)
            with act.Fori(0, QT) as t:
                q = (QT - 1) - t
                with act.If((live & ((2 << q) - 1)) > 0):
                    with act.If(t > 0):
                        null_evacuate(t)
                        for j in range(PAIRS):
                            q_evacuate(t, j)
                            if j < NB:
                                start_output(t, j)
                    with act.Fori(0, q + 1) as back:
                        k = (q - back).with_bounds(min_val=0, max_val=QT - 1)
                        with act.If(((live >> k) & 1) > 0):
                            j = act.snap(jobs, min_val=0, max_val=QT * QT)
                            act.wait_ge(kv_ready, j + 1)
                            act.wait_ge(tiles_set, 2)
                            act.activation(kz[0:DH, :, 0, :], pt_ps[0][0:DH, :].rearrange("p (b t) -> p b t", b=NB),
                                           ACT.Copy).then_inc(kv_evac, 1)
                            act.activation(kz[DH:P, :, 1, :], pt_ps[0][DH:P, :].rearrange("p (b t) -> p b t", b=NB),
                                           ACT.Copy).then_inc(kv_evac, 1)
                            act.activation(vt[:, :, :].rearrange("p b t -> p (b t)"), pt_ps[1][0:DH, :],
                                           ACT.Copy).then_inc(kv_evac, 1)
                            act.wait_ge(v_ready, j + 1)
                            act.activation(v1[:, :, 0:DH], pt_ps[0][:, 0:NB * DH]
                                           .rearrange("p (b d) -> p b d", b=NB), ACT.Copy).then_inc(v_evac, 1)
                            for b in range(NB):
                                def probs(g):
                                    for h in range(g * HG, (g + 1) * HG):
                                        ins = act.activation(ssb[:, b % 2, h, :], ssb[:, b % 2, h, :], ACT.Exp,
                                                             bias=mneg[:, b, h:h + 1])
                                    ins.then_inc(p_done, 1)

                                def transposed(g):
                                    act.wait_ge(pt_ready, 1 + j * NW + b * NG + g + 1)
                                    act.activation(pt[:, g % 2, :, :].rearrange("p h t -> p (h t)"),
                                                   pt_ps[g % 2][:, :], ACT.Copy).then_inc(pt_evac, 1)

                                act.wait_ge(m_new, j * NB + b + 1)
                                act.activation(alpha[:, b % 2, :], dm[:, b % 2, :], ACT.Exp).then_inc(alpha_done, 1)
                                probs(0)
                                for g in range(1, NG):
                                    probs(g)
                                    transposed(g - 1)
                                transposed(NG - 1)
                            act.reg_add(jobs, jobs, 1)
                    for b in range(NB):
                        for i in range(2):
                            act.wait_ge(ot_ready, t * (2 * NB) + 2 * b + i + 1)
                            act.activation(ssb[:, 1, 8 * (b % 2) + 4 * i:8 * (b % 2) + 4 * i + 4, :]
                                           .rearrange("p h t -> p (h t)"), pt_ps[i][:, :], ACT.Copy)\
                                .then_inc(ot_evac, 1)

        @block.vector
        def _(dve):
            chain = [0]

            def link(ins):
                chain[0] += 1
                ins.then_inc(dve_chain, 1)
                dve.wait_ge(dve_chain, chain[0])

            dve.sem_inc(u_free, CREDIT)
            dve.sem_inc(hul_done, CREDIT)
            dve.sem_inc(wb_free, 1)
            dve.wait_ge(small_tr, 1)
            link(dve.tensor_copy(wtT[:, :, :].rearrange("p k e -> p (k e)"), misc_ps[:, 0:KB * 8]))
            link(dve.tensor_copy(wgT[:, :], misc_ps[0:G, 16:24]))
            link(dve.tensor_copy(condT[:, :], misc_ps[:, 24:28]))
            for b in range(NB):
                link(dve.tensor_copy(gcol[:, b, :], condT[0:G, b:b + 1].to_broadcast([G, P])))
            link(dve.tensor_copy(nvc[:, :], condT[:, 1:2].to_broadcast([P, P])))
            dve.memset(nv1[:, DH:D1], 1.0).then_inc(small_ev, 1)
            for c in range(NC):
                cols = slice(c * S, (c + 1) * S)
                dve.wait_ge(xt_ev, KB * (c + 1))
                dve.tensor_copy(xth[:, :, cols], xtf[:, c % 2, :, :]).then_inc(xt_high, 1)
                dve.wait_ge(xt_high, c + 1)
                dve.tensor_tensor(xtl[:, :, cols], xtf[:, c % 2, :, :], xth[:, :, cols].bitcast(F32),
                                  ALU.subtract).then_inc(xt_low, 1)

            full = [P, NT, E]
            e_, c_, k_, o_ = rt
            dve.wait_ge(routed, NC)
            link(dve.tensor_copy(glog[:, :, :].rearrange("p b e -> p (b e)"), wb_ps[:, NT * E:(NT + NB) * E]))
            link(dve.tensor_tensor(c_[:, :, :].rearrange("p (c b) e -> p c (b e)", b=NB),
                                   wb_ps[:, 0:NT * E].rearrange("p (c n) -> p c n", c=NC),
                                   glog[:, :, :].rearrange("p b e -> p (b e)").unsqueeze(1)
                                   .to_broadcast([P, NC, NB * E]), ALU.add))
            link(dve.reduce_max(r1[0][:, :, 0], c_[:, :, :], AX_X))
            link(dve.tensor_tensor(c_[:, :, :], c_[:, :, :], r1[0][:, :, :].to_broadcast(full), ALU.subtract))
            assert chain[0] == CENTRED, chain[0]

            def scores():
                dve.wait_ge(routed, NC + 1)
                link(dve.reduce_sum(r1[0][:, :, 0], c_[:, :, :], AX_X))
                link(dve.reciprocal(r1[0][:, :, :], r1[0][:, :, :]))
                link(dve.tensor_tensor(e_[:, :, :], c_[:, :, :], r1[0][:, :, :].to_broadcast(full), ALU.mult))

            def best(src, hot, top):
                link(dve.reduce_max(top[:, :, 0], src[:, :, :], AX_X))
                link(dve.tensor_tensor(k_[:, :, :], src[:, :, :], top[:, :, :].to_broadcast(full), ALU.is_equal))
                link(dve.tensor_tensor(k_[:, :, :], k_[:, :, :], desc[:, :, :], ALU.mult))
                link(dve.reduce_max(r1[3][:, :, 0], k_[:, :, :], AX_X))
                link(dve.tensor_tensor(hot[:, :, :], k_[:, :, :], r1[3][:, :, :].to_broadcast(full), ALU.is_equal))

            def first_choice():
                dve.wait_ge(consts, 3)
                best(e_, o_, r1[1])
                link(dve.scalar_tensor_tensor(out=c_[:, :, :], in0=o_[:, :, :], scalar=-2.0, in1=e_[:, :, :],
                                              op0=ALU.mult, op1=ALU.add))

            def second_choice():
                best(c_, c_, r1[2])

            def routing_weights():
                link(dve.tensor_tensor(o_[:, :, :], o_[:, :, :], c_[:, :, :], ALU.add))
                link(dve.tensor_tensor(e_[:, :, :], e_[:, :, :], o_[:, :, :], ALU.mult))
                link(dve.tensor_tensor(r1[1][:, :, :], r1[1][:, :, :], r1[2][:, :, :], ALU.add))
                link(dve.tensor_scalar(r1[1][:, :, :], r1[1][:, :, :], 1e-20, None, ALU.add))
                link(dve.reciprocal(r1[1][:, :, :], r1[1][:, :, :]))
                link(dve.tensor_tensor(e_[:, :, :], e_[:, :, :], r1[1][:, :, :].to_broadcast(full), ALU.mult))
                link(dve.tensor_copy(w3[:, :, 0, :], e_[:, :, :]))
                link(dve.tensor_tensor(c_[:, :, :], e_[:, :, :], w3[:, :, 0, :], ALU.subtract))
                link(dve.tensor_copy(w3[:, :, 1, :], c_[:, :, :]))
                link(dve.tensor_tensor(e_[:, :, :], c_[:, :, :], w3[:, :, 1, :], ALU.subtract))
                dve.tensor_copy(w3[:, :, 2, :], e_[:, :, :]).then_inc(w3_ready, 1)

            def weights_kept():
                dve.wait_ge(w3_tr, 1)
                dve.tensor_copy(w3t[:, 0:NT * P // 2], wb_ps[0:3 * E, :].bitcast(BF16)).then_inc(w3_ev, 1)
                dve.wait_ge(w3_tr, 2)
                dve.tensor_copy(w3t[:, NT * P // 2:NT * P], misc_ps[0:3 * E, :].bitcast(BF16)).then_inc(m_free, 1)

            def mask_and_live():
                dve.wait_ge(mask_in, 16)
                link(dve.tensor_scalar(maskb[:, :], masku[:, :], -1.0, BIG, ALU.add, ALU.mult))
                link(dve.tensor_reduce(live4[:, :], masku[:, :].rearrange("o (b k s) -> o k b s", b=NB, k=QT),
                                       AX_XY, ALU.max))
                link(dve.tensor_tensor(live4[:, :], live4[:, :], pow2[:, :], ALU.mult))
                link(dve.reduce_sum(livew[:, :], live4[:, :], AX_X))
                dve.tensor_copy(livei[:, :], livew[:, :]).then_inc(live_done, 1)

            def unit_low(b, s):
                dve.wait_ge(huh_done, b * NU + s + 1)
                dve.tensor_tensor(hul[:, s % 2, :], hid[:, s % 2, :], huh[:, s % 2, :].bitcast(F32), ALU.subtract)\
                    .then_inc(hul_done, 1)

            def null_row():
                dve.wait_ge(oc_ready, 1)
                dve.tensor_copy(oc[:, :], misc_ps[:, 0:H]).then_inc(m_free, 1)
                dve.wait_ge(m_free, 2)
                dve.bn_stats(st6[:, 0, :], oc[:, :]).then_inc(oc_stat, 1)
                dve.wait_ge(oc_stat, 1)
                dve.bn_aggr(mv[:, 0, :], st6[:, 0, :]).then_inc(oc_mv, 1)
                dve.wait_ge(oc_rstd, 1)
                dve.tensor_scalar(oc[:, :], oc[:, :], mv[:, 0, 0:1], rstd[:, 0:1], ALU.subtract, ALU.mult)\
                    .then_inc(oc_norm, 1)
                dve.wait_ge(oc_norm, 1)
                dve.wait_ge(vec_in, 80)
                dve.tensor_tensor(oc[:, :], oc[:, :], gout[:, :], ALU.mult).then_inc(oc_done, 1)

            def null_weights():
                dve.wait_ge(wn_multiplied, 1)
                dve.reduce_sum(wnf[:, :, :].rearrange("p k h -> p (k h)"), wn_products, AX_X).then_inc(wn_summed, 1)
                dve.wait_ge(wn_summed, 1)
                dve.tensor_copy(wnh[:, :, :], wnf[:, :, :]).then_inc(wn_done, 1)
                dve.wait_ge(wn_done, 1)
                dve.tensor_tensor(wnl[:, :, :], wnf[:, :, :], wnh[:, :, :].bitcast(F32), ALU.subtract)\
                    .then_inc(wn_done, 1)

            def add_moe(b, i):
                dve.wait_ge(m_ready, b * 4 + 1 + i)
                rows = xtok[:, bass.ds(b * QT + 2 * i, 2), :]
                dve.tensor_tensor(rows, rows, misc_ps[:, :].rearrange("p (t h) -> p t h", t=2), ALU.add)\
                    .then_inc(m_free, 1)

            def stats(b):
                wait_apart(dve, m_free, OC_M + b * 4 + 2)
                for t in range(QT):
                    dve.bn_stats(st6[:, t, :], xtok[:, bass.ds(b * QT + t, 1), :]
                                 .rearrange("p a h -> p (a h)")).then_inc(st_done, 1)
                wait_apart(dve, st_done, (b + 1) * QT)
                for t in range(QT):
                    dve.bn_aggr(mv[:, t, :], st6[:, t, :]).then_inc(mv_done, 1)

            def normalise(b):
                dve.wait_ge(rstd_done, b + 1)
                for t in range(QT):
                    dve.tensor_scalar(xn[:, t, :], xtok[:, bass.ds(b * QT + t, 1), :].rearrange("p a h -> p (a h)"),
                                      mv[:, t, 0:1], rstd[:, t:t + 1], ALU.subtract, ALU.mult).then_inc(xn_done, 1)

            def split_xn(b, k):
                dve.wait_ge(m_free, OC_M + b * 4 + 3 + k)
                dst = xth[:, k, bass.ds(b * S, S)]
                dve.tensor_copy(dst, yt[:, k, :]).then_inc(xnh_done, 1)
                dve.wait_ge(xnh_done, b * 2 + k + 1)
                dve.tensor_tensor(xtl[:, k, bass.ds(b * S, S)], yt[:, k, :], dst.bitcast(F32), ALU.subtract)\
                    .then_inc(xnl_done, 1)

            def experts(b, first):
                for s in range(NU):
                    n = b * NU + s
                    if s >= 1:
                        unit_low(b, s - 1)
                    elif not first:
                        unit_low(b - 1, NU - 1)
                    if first and s == 1:
                        first_choice()
                    if first and s == NSH:
                        routing_weights()
                        weights_kept()
                    dve.wait_ge(g_free, n + 1 + CREDIT)
                    dve.scalar_tensor_tensor(out=hid[:, s % 2, :], in0=hid[:, s % 2, :], scalar=LEAK,
                                             in1=hid[:, s % 2, :], op0=ALU.mult, op1=ALU.max).then_inc(leaked, 1)
                    dve.wait_ge(leaked, n + 1)
                    if s >= NSH:
                        r = b * E + s - NSH
                        dve.wait_ge(wb_ready, r + 1)
                        dve.tensor_tensor(hid[:, s % 2, :], hid[:, s % 2, :], wb_ps[:, :], ALU.mult)\
                            .then_inc(wb_free, 1)
                        dve.wait_ge(wb_free, r + 2)
                    dve.wait_ge(u_ready, n + 1)
                    dve.tensor_tensor(hid[:, s % 2, :], hid[:, s % 2, :], up_ps[s % 2][:, :], ALU.mult)\
                        .then_inc(u_free, 1)
                    if first and s == 0:
                        scores()
                    if first and s == 1:
                        second_choice()
                    if first and s == NU // 2:
                        mask_and_live()
                    if first and s == NU - 1:
                        null_row()
                    if first and s == NU - 2:
                        null_weights()
                    if not first:
                        if s in (2, 3):
                            add_moe(b - 1, s - 2)
                        if s == 4:
                            stats(b - 1)
                        if s == 5:
                            normalise(b - 1)
                        if s in (6, 7):
                            split_xn(b - 1, s - 6)

            experts(0, True)
            with dve.Fori(1, NC) as b:
                experts(b, False)
            unit_low(NC - 1, NU - 1)
            for i in range(2):
                add_moe(NC - 1, i)
            stats(NC - 1)
            normalise(NC - 1)
            for k in range(KB):
                split_xn(NC - 1, k)

            live = dve.value_load(livei[0:1, 0:1], min_val=0, max_val=2 ** QT - 1)
            jobs = dve.alloc_register("dve_jobs")
            dve.reg_mov(jobs, 0)
            with dve.Fori(0, QT) as t:
                q = (QT - 1) - t
                with dve.If((live & ((2 << q) - 1)) > 0):
                    dve.wait_ge(null_tr, t + 1)
                    dve.scalar_tensor_tensor(out=mneg[:, :, :], scalar=-1.0,
                                             in0=proj_ps[0][:, 0:NB * NH].rearrange("p (b h) -> p b h", b=NB),
                                             in1=nbias[:, :].unsqueeze(1).to_broadcast([P, NB, NH]),
                                             op0=ALU.mult, op1=ALU.subtract).then_inc(m_init, 1)
                    with dve.Fori(0, q + 1) as back:
                        k = (q - back).with_bounds(min_val=0, max_val=QT - 1)
                        with dve.If(((live >> k) & 1) > 0):
                            j = dve.snap(jobs, min_val=0, max_val=QT * QT)

                            def gather(b):
                                for g in range(NG):
                                    dve.wait_ge(pv_ready, j * NW + b * NG + g + 1)
                                    if g == 0:
                                        dve.wait_ge(o_scaled, j * NB + b + 1)
                                    hs = slice(g * HG, (g + 1) * HG)
                                    dve.tensor_tensor(ost[:, b, hs, :], ost[:, b, hs, :],
                                                      pv_ps[g % 2][:, 0:HG * D1].rearrange("p (h d) -> p h d", h=HG),
                                                      ALU.add).then_inc(o_added, 1)

                            dve.wait_ge(bias_masked, j + 1)
                            for b in range(NB):
                                for g in range(NG):
                                    dve.wait_ge(s_ready, j * NW + b * NG + g + 1)
                                    if g == 0:
                                        if b >= 2:
                                            dve.wait_ge(pt_ready, 1 + j * NW + (b - 1) * NG)
                                        else:
                                            dve.wait_ge(pt_ready, 1 + j * NW)
                                            dve.wait_ge(wo_ready, 1 + t * NB)
                                    hs = slice(g * HG, (g + 1) * HG)
                                    dve.tensor_tensor(ssb[:, b % 2, hs, :],
                                                      s_ps[g][:, :].rearrange("p (h k) -> p h k", h=HG),
                                                      bias[:, hs, :], ALU.add).then_inc(s_added, 1)
                                dve.wait_ge(s_added, 1 + j * NW + (b + 1) * NG)
                                dve.reduce_max(mx[:, :], ssb[:, b % 2, :, :], AX_X).then_inc(s_max, 1)
                                dve.wait_ge(s_max, j * NB + b + 1)
                                dve.wait_ge(m_init, t + 1)
                                dve.scalar_tensor_tensor(out=mx[:, :], in0=mx[:, :], scalar=-1.0, in1=mneg[:, b, :],
                                                         op0=ALU.mult, op1=ALU.min).then_inc(m_step, 1)
                                dve.wait_ge(m_step, j * NB + b + 1)
                                if b < 2:
                                    dve.wait_ge(alpha_done, 1 + j * NB)
                                else:
                                    dve.wait_ge(alpha_done, 1 + j * NB + b - 1)
                                dve.tensor_tensor(dm[:, b % 2, :], mx[:, :], mneg[:, b, :], ALU.subtract)\
                                    .then_inc(m_delta, 1)
                                dve.wait_ge(m_delta, j * NB + b + 1)
                                dve.tensor_copy(mneg[:, b, :], mx[:, :]).then_inc(m_new, 1)
                                if b >= 1:
                                    gather(b - 1)
                            gather(NB - 1)
                            dve.reg_add(jobs, jobs, 1)

                    j = dve.snap(jobs, min_val=0, max_val=QT * QT)
                    dve.wait_ge(o_added, 1 + j * NW)
                    for b in range(NB):
                        n = t * NB + b
                        if b == 0:
                            dve.wait_ge(on_done, 1 + n)
                        dve.reciprocal(rl[:, b, :], ost[:, b, :, DH]).then_inc(rl_done, 1)
                        dve.wait_ge(rl_done, n + 1)
                        if b >= 2:
                            dve.wait_ge(ot_ready, 2 * (n - 1))
                        else:
                            dve.wait_ge(pt_ready, 1 + j * NW)
                        dve.tensor_tensor(ssb[:, 0, 8 * (b % 2):8 * (b % 2) + 8, :]
                                          .rearrange("p a (c d) -> p (a c) d", d=DH),
                                          ost[:, b, :, 0:DH], rl[:, b, :].unsqueeze(2).to_broadcast([P, NH, DH]),
                                          ALU.mult).then_inc(on_done, 1)
                    for b in range(NB):
                        n = t * NB + b
                        acc = pv_ps[b % 2][:, 0:H]
                        dve.wait_ge(wo_ready, 1 + n + 1)
                        dve.bn_stats(st6[:, b, :], acc).then_inc(ln_stat, 1)
                        wait_apart(dve, ln_stat, n + 1)
                        dve.bn_aggr(mv[:, b, :], st6[:, b, :]).then_inc(ln_mv, 1)
                        dve.wait_ge(ln_rstd, n + 1)
                        if b == 0:
                            dve.wait_ge(row_out, 1 + t * (16 * NB))
                            dve.wait_ge(ob_out, 1 + 16 * NC)
                        dve.tensor_scalar(obuf[:, b, :], acc, mv[:, b, 0:1], rstd[:, b:b + 1],
                                          ALU.subtract, ALU.mult).then_inc(ln_norm, 1)
                        dve.wait_ge(ln_norm, 1 + n + 1)
                        dve.tensor_tensor(obuf[:, b, :], obuf[:, b, :], gout[:, :], ALU.mult).then_inc(ln_scale, 1)
                        dve.wait_ge(ln_scale, n + 1)
                        dve.tensor_tensor(obuf[:, b, :], obuf[:, b, :],
                                          xtok[:, bass.ds(chunk_of(q) * NB + b, 1), :].rearrange("p a h -> p (a h)"),
                                          ALU.add).then_inc(row_done, 1)

        @block.tensor
        def _(pe):
            mm = nc.tensor.matmul
            tr = nc.tensor.transpose
            pe.sem_inc(down_done, CREDIT)
            pe.wait_ge(consts, 2)
            pe.wait_ge(small_in, 64)
            for k in range(KB):
                tr(misc_ps[:, 8 * k:8 * k + 8], small[:, k * P:(k + 1) * P], ident[0:8, 0:8])
            tr(misc_ps[0:G, 16:24], small[:, H:H + G], ident[0:8, 0:8])
            tr(misc_ps[:, 24:28], small[0:NB, H + P:H + 2 * P], ident[0:NB, 0:NB]).then_inc(small_tr, 1)

            def x_transposes(c):
                pe.wait_ge(x_in[c], 16)
                for k in range(KB):
                    if c >= 2:
                        pe.wait_ge(xt_ev, KB * (c - 2) + k + 1)
                    for b in range(NB):
                        ins = tr(bank[2 * (c % 2) + k][:, b * P:(b + 1) * P],
                                 xtok[:, c * NB + b, k * P:(k + 1) * P], ident[:, :])
                    ins.then_inc(xt_tr, 1)

            def router(c):
                pe.wait_ge(xt_ev, KB * (c + 1))
                for b in range(NB):
                    acc = wb_ps[:, (c * NB + b) * E:(c * NB + b + 1) * E]
                    for k in range(KB):
                        ins = mm(acc, xtf[:, c % 2, k, b * P:(b + 1) * P], wtT[:, k, :],
                                 start=(k == 0), stop=(k == KB - 1))
                ins.then_inc(routed, 1)

            x_transposes(0)
            x_transposes(1)
            pe.wait_ge(small_ev, 1)
            for b in range(NB):
                mm(wb_ps[:, (NT + b) * E:(NT + b + 1) * E], gcol[:, b, :], wgT[:, :], start=True, stop=True)
            for c in range(NC):
                router(c)
                if c + 2 < NC:
                    x_transposes(c + 2)

            def weights_transposed():
                pe.wait_ge(w3_ready, 1)
                for i, dst in enumerate((wb_ps, misc_ps)):
                    view = dst[0:3 * E, :].bitcast(BF16)
                    for n in range(NT // 2):
                        ins = tr(view[:, n * P:(n + 1) * P],
                                 w3[:, i * NT // 2 + n, :, :].rearrange("p k e -> p (k e)"), identb[:, :])
                    ins.then_inc(w3_tr, 1)
                pe.wait_ge(w3_ev, 1)
                pe.wait_ge(m_free, 1)

            def down(b, s):
                n = b * NU + s
                pe.wait_ge(hul_done, n + 1 + CREDIT)
                if s == 0:
                    pe.wait_ge(y_free, CREDIT + b * KB)
                for k in range(KB):
                    cols = slice(k * P, (k + 1) * P)
                    ins = split3(mm, y_ps[k][:, :], wh[:, s, 2, cols], wl[:, s, 2, cols],
                                 huh[:, s % 2, :], hul[:, s % 2, :], s == 0, s == NU - 1)
                ins.then_inc(down_done, 1)

            def spread_weight(b, s):
                wait_apart(pe, wb_free, b * E + s - NSH + 1)
                mm(wb_ps[:, :], sel[:, s - NSH, :], w3t[:, bass.ds(b * S, S)], start=True, stop=True)\
                    .then_inc(wb_ready, 1)

            def null_row():
                pe.wait_ge(wo_in, 16)
                pe.wait_ge(m_free, 1)
                for j in range(PAIRS):
                    ins = mm(misc_ps[:, 0:H], nvc[:, :], wo[:, j, :], start=(j == 0), stop=(j == PAIRS - 1))
                ins.then_inc(oc_ready, 1)

            def moe_rows(b, i):
                pe.wait_ge(y_free, CREDIT + (b + 1) * KB)
                pe.wait_ge(m_free, OC_M + b * 4 + i)
                for t in range(2):
                    for k in range(KB):
                        ins = tr(misc_ps[:, t * H + k * P:t * H + (k + 1) * P],
                                 yt[:, k, (2 * i + t) * P:(2 * i + t + 1) * P], ident[:, :])
                ins.then_inc(m_ready, 1)

            def xn_cols(b, k):
                pe.wait_ge(xn_done, (b + 1) * QT)
                pe.wait_ge(m_free, OC_M + b * 4 + 2 + k)
                for t in range(QT):
                    ins = tr(misc_ps[:, t * P:(t + 1) * P], xn[:, t, k * P:(k + 1) * P], ident[:, :])
                ins.then_inc(m_ready, 1)

            def experts(b, first):
                for s in range(NU):
                    n = b * NU + s

                    def product(acc, kind):
                        for k in range(KB):
                            cols = slice(k * M, (k + 1) * M)
                            ins = split3(mm, acc, wh[:, s, kind, cols], wl[:, s, kind, cols],
                                         xth[:, k, bass.ds(b * S, S)], xtl[:, k, bass.ds(b * S, S)],
                                         k == 0, k == KB - 1)
                        return ins

                    if first:
                        pe.wait_ge(wl_done, s + 1)
                        if s == 0:
                            pe.wait_ge(xt_low, 1)
                    pe.wait_ge(g_free, n + 1)
                    product(gate_ps[s % 2][:, :], 0).then_inc(g_ready, 1)
                    routed_late = first and s == NSH
                    if s >= NSH and not routed_late:
                        spread_weight(b, s)
                    pe.wait_ge(u_free, n + 1)
                    product(up_ps[s % 2][:, :], 1).then_inc(u_ready, 1)
                    if s >= 1:
                        down(b, s - 1)
                    elif not first:
                        down(b - 1, NU - 1)
                    if routed_late:
                        weights_transposed()
                        spread_weight(b, s)
                    if first and s == NU - 1:
                        pe.wait_ge(xt_low, NC)
                        null_row()
                    if not first:
                        if s in (2, 3):
                            moe_rows(b - 1, s - 2)
                        if s in (6, 7):
                            xn_cols(b - 1, s - 6)

            experts(0, True)
            with pe.Fori(1, NC) as b:
                experts(b, False)
            pe.wait_ge(live_done, 1)
            live = pe.value_load(livei[0:1, 0:1], min_val=0, max_val=2 ** QT - 1)
            jobs = pe.alloc_register("pe_jobs")
            pe.reg_mov(jobs, 0)
            down(NC - 1, NU - 1)

            def project(acc, high, low, tile):
                first_col = chunk_of(tile) * S
                for k in range(KB):
                    ins = split3(mm, acc, high(k), low(k), xth[:, k, bass.ds(first_col, S)],
                                 xtl[:, k, bass.ds(first_col, S)], k == 0, k == KB - 1)
                return ins

            def q_project(t, j):
                if isinstance(t, int) and j < 2:
                    pe.wait_ge(g_free, TOT + CREDIT)
                if j >= 2:
                    pe.wait_ge(q_evac, t * PAIRS + j - 1)
                project(logit_ps[j % 2][:, :], lambda k: wqh[:, k, j * P:(j + 1) * P],
                        lambda k: wql[:, k, j * P:(j + 1) * P], (QT - 1) - t).then_inc(q_ready, 1)

            def null_project(t):
                project(proj_ps[0][0:NH, :], lambda k: wnh[:, k, :], lambda k: wnl[:, k, :], (QT - 1) - t)\
                    .then_inc(null_ready, 1)

            def null_transposes(t):
                wait_apart(pe, null_evac, t + 1)
                for b in range(NB):
                    ins = tr(proj_ps[0][:, b * NH:(b + 1) * NH], null_t[:, b, :], ident[0:NH, 0:NH])
                ins.then_inc(null_tr, 1)

            pe.wait_ge(wql_done, 2)
            pe.wait_ge(wn_done, 2)
            pe.wait_ge(wb_free, 1 + NC * E)
            null_project(0)
            for j in range(PAIRS):
                q_project(0, j)
                if j == 0:
                    moe_rows(NC - 1, 0)
                if j == 1:
                    moe_rows(NC - 1, 1)
                if j == PAIRS - 2:
                    xn_cols(NC - 1, 0)
            xn_cols(NC - 1, 1)

            pe.wait_ge(m_free, OC_M + 4 * NC)
            pe.wait_ge(u_free, TOT + CREDIT)

            with pe.Fori(0, QT) as t:
                q = (QT - 1) - t
                with pe.If((live & ((2 << q) - 1)) > 0):
                    with pe.If(t > 0):
                        j = pe.snap(jobs, min_val=0, max_val=QT * QT)
                        pe.wait_ge(s_added, 1 + j * NW)
                        null_project(t)
                        for j in range(PAIRS):
                            q_project(t, j)
                    null_transposes(t)
                    wait_apart(pe, q_evac, (t + 1) * PAIRS)
                    with pe.Fori(0, q + 1) as back:
                        k = (q - back).with_bounds(min_val=0, max_val=QT - 1)
                        with pe.If(((live >> k) & 1) > 0):
                            j = pe.snap(jobs, min_val=0, max_val=QT * QT)
                            pe.wait_ge(pt_evac, 1 + j * NW)
                            pe.wait_ge(xnl_done, (chunk_of(k) + 1) * KB)
                            project(pt_ps[0][:, :], lambda kk: wkvh[:, kk, DH:3 * DH],
                                    lambda kk: wkvl[:, kk, DH:3 * DH], k)
                            project(pt_ps[1][:, :], lambda kk: wkvh[:, kk, 0:2 * DH],
                                    lambda kk: wkvl[:, kk, 0:2 * DH], k).then_inc(kv_ready, 1)
                            wait_apart(pe, kv_evac, j * 3 + 3)
                            for b in range(NB):
                                ins = tr(pt_ps[0][:, b * DH:(b + 1) * DH], vt[:, b, :], ident[0:DH, 0:DH])
                            ins.then_inc(v_ready, 1)
                            wait_apart(pe, m_init, t + 1)

                            def logits(b, g):
                                w = j * NW + b * NG + g
                                acc = s_ps[g]
                                wait_apart(pe, s_added, 1 + (w - NG + 1 if b > 0 else j * NW))
                                mm(acc[:, :].rearrange("p (h k) -> p h k", h=HG), onesb[:, :],
                                   mask_q[:, b:b + 1, bass.ds(k * P, P)].to_broadcast([1, HG, P]),
                                   start=True, stop=False)
                                for i in range(2):
                                    ins = mm(acc[:, i * 2 * P:(i + 1) * 2 * P], qt_sb[:, 2 * g + i, b, :],
                                             kz[:, b, :, :].rearrange("p a k -> p (a k)"),
                                             start=False, stop=(i == 1))
                                ins.then_inc(s_ready, 1)

                            def transposes(b, g):
                                w = b * NG + g
                                pe.wait_ge(p_done, j * NW + w + 1)
                                pe.wait_ge(pt_evac, 1 + j * NW + max(w - 1, 0))
                                for i in range(HG):
                                    ins = tr(pt_ps[g % 2][:, i * P:(i + 1) * P], ssb[:, b % 2, g * HG + i, :],
                                             ident[:, :])
                                ins.then_inc(pt_ready, 1)

                            def values(b, g):
                                w = b * NG + g
                                pe.wait_ge(pt_evac, 1 + j * NW + w + 1)
                                pe.wait_ge(o_added, 1 + j * NW + max(w - 1, 0))
                                for i in range(HG):
                                    ins = mm(pv_ps[g % 2][:, i * D1:(i + 1) * D1], pt[:, g % 2, i, :], v1[:, b, :],
                                             start=True, stop=True)
                                ins.then_inc(pv_ready, 1)

                            def weighted(b):
                                if b == 0:
                                    wait_apart(pe, v_evac, 1 + j + 1)
                                transposes(b, 0)
                                for g in range(1, NG):
                                    transposes(b, g)
                                    values(b, g - 1)
                                values(b, NG - 1)

                            pe.wait_ge(ln_norm, 1 + t * NB)
                            for b in range(NB):
                                for g in range(NG):
                                    logits(b, g)
                                if b >= 1:
                                    weighted(b - 1)
                            weighted(NB - 1)
                            pe.reg_add(jobs, jobs, 1)

                    j = pe.snap(jobs, min_val=0, max_val=QT * QT)
                    pe.wait_ge(pt_evac, 1 + j * NW)
                    pe.wait_ge(o_added, 1 + j * NW)

                    def out_transposes(b):
                        n = t * NB + b
                        pe.wait_ge(on_done, 1 + n + 1)
                        for i in range(2):
                            if b >= 1:
                                pe.wait_ge(ot_evac, 2 * (n - 1) + i + 1)
                            for c in range(4):
                                ins = tr(pt_ps[i][:, c * P:(c + 1) * P], ssb[:, 0, 8 * (b % 2) + 4 * i + c, :],
                                         ident[:, :])
                            ins.then_inc(ot_ready, 1)

                    def out_project(b):
                        n = t * NB + b
                        pe.wait_ge(ot_evac, 2 * (n + 1))
                        if b >= 2:
                            pe.wait_ge(ln_norm, 1 + n - 1)
                        for jj in range(PAIRS):
                            ins = mm(pv_ps[b % 2][:, 0:H], ssb[:, 1, 8 * (b % 2) + jj, :], wo[:, jj, :],
                                     start=(jj == 0), stop=(jj == PAIRS - 1))
                        ins.then_inc(wo_ready, 1)

                    out_transposes(0)
                    for b in range(1, NB):
                        out_transposes(b)
                        out_project(b - 1)
                    out_project(NB - 1)


CENTRED = 12


_INS = ["x", "cond_64", "fside_16xSxS_0", "mask_BxS_bk0", "L0_cond_wt", "L0_cond_wg", "L0_cond_w_gate",
        "L0_cond_w_up", "L0_cond_w_down", "L0_cond_sw_gate", "L0_cond_sw_up", "L0_cond_sw_down", "L1_cond_g_in",
        "L1_cond_null_attn_bias", "L1_cond_Wq", "L1_cond_Wkv", "L1_cond_Wo", "L1_cond_g_out"]


def kernel(**inputs):
    import numpy as _np
    import concourse.bacc as _bacc
    from concourse import mybir as _mybir
    from concourse.bass_utils import run_bass_kernel_spmd as _run

    nc = _bacc.Bacc("TRN2", target_bir_lowering=False, num_devices=1)
    arrays, args = {}, []
    for name in _INS:
        a = _np.ascontiguousarray(inputs[name])
        arrays[f"in_{name}"] = a
        args.append(nc.dram_tensor(f"in_{name}", a.shape, _mybir.dt.from_np(a.dtype), kind="ExternalInput").ap())
    shape = inputs["x"].shape
    args.append(nc.dram_tensor("out_x", shape, _mybir.dt.float32, kind="ExternalOutput").ap())
    moe_then_attention(nc, *args)
    r = _run(nc, [arrays], core_ids=[0])
    return r.results[0]["out_x"]
```

```python
from contextlib import ExitStack

import concourse.bass as bass
from concourse import mybir

P = 128
F32 = mybir.dt.float32
F32R = mybir.dt.float32r
BF16 = mybir.dt.bfloat16
U8 = mybir.dt.uint8
I32 = mybir.dt.int32
ALU = mybir.AluOpType
ACT = mybir.ActivationFunctionType
AX_X = mybir.AxisListType.X
AX_XY = mybir.AxisListType.XY

BIG = 1e30
EPS = 1e-5
LEAK = 0.01
CREDIT = 2


def moe_then_attention(nc, x, cond, fside, mask, wt, wg, w_gate, w_up, w_down, sw_gate, sw_up, sw_down,
                       g_in, null_bias, w_q, w_kv, w_o, g_out, out):
    NB, S, H = x.shape
    E = w_gate.shape[0]
    M = w_gate.shape[2]
    NSH = sw_gate.shape[1] // M
    NU = NSH + E
    G = cond.shape[1]
    NH = fside.shape[0]
    INNER = w_q.shape[1]
    DH = INNER // NH
    KB = H // P
    QT = S // P
    NT = NB * QT
    NC = QT
    PAIRS = NH // 2
    HG = 4
    NG = NH // HG
    D1 = DH + 1
    NW = NB * NG
    assert M == P and S == 512 and KB == 2 and DH == 64 and NB == QT == 4 and NSH == 2 and NU % 2 == 0 and G == DH

    with ExitStack() as ctx:
        def sb(name, shape, dt=F32):
            return ctx.enter_context(nc.sbuf_tensor(name, shape, dt))

        def sem(name):
            return ctx.enter_context(nc.semaphore(name))

        bank = [ctx.enter_context(nc.psum_tensor(f"bank{i}", [P, 512], F32)) for i in range(8)]
        gate_ps, up_ps, wb_ps, y_ps, misc_ps = bank[0:2], bank[2:4], bank[4], bank[5:7], bank[7]
        logit_ps, pt_ps, pv_ps, proj_ps = bank[0:2], bank[2:4], bank[5:7], (bank[4], bank[7])
        s_ps = (*logit_ps, *proj_ps)

        xtok = sb("xtok", [P, NT, H])
        xtf = sb("xtf", [P, 2, KB, S])
        xth = sb("xth", [P, KB, NB * S], F32R)
        xtl = sb("xtl", [P, KB, NB * S], F32R)
        wraw = sb("wraw", [P, NU * 3 * 256])
        wqh = sb("wqh", [P, KB, INNER], F32R)
        wql = sb("wql", [P, KB, INNER], F32R)
        wkvh = sb("wkvh", [P, KB, 3 * DH], F32R)
        wkvl = sb("wkvl", [P, KB, 3 * DH], F32R)
        wo = sb("wo", [P, PAIRS, H])
        hid = sb("hid", [P, 2, S])
        huh = sb("huh", [P, 2, S], F32R)
        hul = sb("hul", [P, 2, S], F32R)
        obuf = sb("obuf", [P, QT, H])
        ident = sb("ident", [P, P])
        identb = sb("identb", [P, P], BF16)
        small = hid[0:8, 1, :]
        wtT = sb("wtT", [P, KB, 8])
        wgT = sb("wgT", [G, 8])
        condT = sb("condT", [P, 4])
        glog = sb("glog", [E, NB])
        nkb = sb("nkb", [P, DH])
        wnf = sb("wnf", [P, KB, NH])
        wnh = sb("wnh", [P, KB, NH], F32R)
        wnl = sb("wnl", [P, KB, NH], F32R)
        nvc = sb("nvc", [P, P])
        nv1 = sb("nv1", [P, D1])
        nbias = sb("nbias", [P, NH])
        gin = sb("gin", [P, KB])
        gout = sb("gout", [P, H])
        oc = sb("oc", [P, H])
        masku = obuf[:, 2:4, :].rearrange("p t h -> p (t h)").bitcast(U8)
        maskb = sb("maskb", [P, NB * S], BF16)
        live4 = sb("live4", [1, QT])
        pow2 = sb("pow2", [1, QT])
        livew = sb("livew", [1, 1])
        livei = sb("livei", [1, 1], I32)
        rt = [obuf[:, i // 2, (i % 2) * NT * E:(i % 2 + 1) * NT * E].rearrange("p (t e) -> p t e", e=E)
              for i in range(4)]
        r1 = [sb(f"r1{i}", [P, NT, 1]) for i in range(4)]
        desc = sb("desc", [P, NT, E])
        w3 = sb("w3", [P, NT, 3, E], BF16)
        w3t = sb("w3t", [3 * E, NT * P], BF16)
        sel = sb("sel", [3 * E, E, P], BF16)
        st6 = sb("st6", [P, QT, 6])
        mv = sb("mv", [P, QT, 2])
        rstd = sb("rstd", [P, QT])
        half = sb("half", [P, QT])
        mx = sb("mx", [P, NH])
        mneg = sb("mneg", [P, NB, NH])
        dm = sb("dm", [P, 2, NH])
        alpha = sb("alpha", [P, 2, NH])
        rl = sb("rl", [P, NB, NH])

        with ExitStack() as early:
            wh = early.enter_context(nc.sbuf_tensor("wh", [P, NU, 3, 256], F32R))
            wl = early.enter_context(nc.sbuf_tensor("wl", [P, NU, 3, 256], F32R))
        qt_sb = sb("qt_sb", [P, PAIRS, NB, P])
        ost = sb("ost", [P, NB, NH, D1])
        kz = sb("kz", [P, NB, 2, P])
        vt = sb("vt", [DH, NB, P])
        v1 = sb("v1", [P, NB, D1])
        ssb = sb("ssb", [P, 2, NH, P])
        pt = sb("pt", [P, 2, HG, P])

        on = hid[:, :, :].rearrange("p a (c d) -> p (a c) d", d=DH)
        null_t = ssb[0:NH, 1, 0:NB, :]
        wn_products = xtf[:, :, :, :].rearrange("p c k s -> p (c k s)").rearrange("p (n d) -> p n d", d=DH)
        wo_sums = xtf[:, 0, :, :].rearrange("p k s -> p (k s)").rearrange("p (j h) -> p j h", h=H)
        wo_sum = oc
        yt = xtf[:, 0, :, :]
        xn = xtf[:, 1, :, :].rearrange("p k (t h) -> p (k t) h", h=H)
        wraw_u = wraw[:, :].rearrange("p (u w n) -> p u w n", u=NU, w=3)
        bias = wraw[:, 0:NH * P].rearrange("p (h k) -> p h k", h=NH)
        wq_raw = wraw[:, NH * P:NH * P + KB * INNER].rearrange("p (k n) -> p k n", k=KB)
        wkv_raw = wraw[:, NH * P + KB * INNER:NH * P + KB * INNER + KB * 3 * DH].rearrange("p (k n) -> p k n", k=KB)
        spare = NH * P + KB * INNER + KB * 3 * DH
        on_t = [wraw[:, spare + i * INNER:spare + (i + 1) * INNER].rearrange("p (a c) -> p a c", a=2)
                for i in range(2)]
        logit_t = w3t[0:E, :].bitcast(F32).rearrange("e (c s) -> e c s", c=2)
        mask_q = maskb[:, :].rearrange("p (b s) -> p b s", b=NB)
        out_t = out.rearrange("b (t p) h -> t p b h", p=P)
        x_t = x.rearrange("b (t p) h -> t p b h", p=P)

        x_in = [sem(f"x_in{b}") for b in range(NB)]
        small_in = sem("small_in")
        w_in = [sem(f"w_in{i}") for i in range(1 + E // 2)]
        wq_in = sem("wq_in")
        wo_in = sem("wo_in")
        vec_in = sem("vec_in")
        mask_in = sem("mask_in")
        zeroed = sem("zeroed")
        consts = sem("consts")
        small_tr = sem("small_tr")
        small_ev = sem("small_ev")
        xt_tr = sem("xt_tr")
        xt_ev = sem("xt_ev")
        xt_high = sem("xt_high")
        xt_low = sem("xt_low")
        glog_ready = sem("glog_ready")
        lt_ready = sem("lt_ready")
        lt_evac = sem("lt_evac")
        routed = sem("routed")
        dve_chain = sem("dve_chain")
        pool_chain = sem("pool_chain")
        w3_ready = sem("w3_ready")
        w3_tr = sem("w3_tr")
        w3_ev = sem("w3_ev")
        wh_done = sem("wh_done")
        wl_done = sem("wl_done")
        wqh_done = sem("wqh_done")
        wql_done = sem("wql_done")
        wn_multiplied = sem("wn_multiplied")
        wn_summed = sem("wn_summed")
        wn_done = sem("wn_done")
        live_done = sem("live_done")
        mask_done = sem("mask_done")
        wo_summed = sem("wo_summed")
        g_ready = sem("g_ready")
        g_free = sem("g_free")
        u_ready = sem("u_ready")
        u_free = sem("u_free")
        wb_ready = sem("wb_ready")
        wb_free = sem("wb_free")
        leaked = sem("leaked")
        huh_done = sem("huh_done")
        hul_done = sem("hul_done")
        down_done = sem("down_done")
        y_free = sem("y_free")
        m_ready = sem("m_ready")
        m_free = sem("m_free")
        oc_ready = sem("oc_ready")
        oc_stat = sem("oc_stat")
        oc_mv = sem("oc_mv")
        oc_done = sem("oc_done")
        st_done = sem("st_done")
        mv_done = sem("mv_done")
        rstd_done = sem("rstd_done")
        xn_done = sem("xn_done")
        xnh_done = sem("xnh_done")
        xnl_done = sem("xnl_done")
        ob_ready = sem("ob_ready")
        ob_out = sem("ob_out")
        tiles_set = sem("tiles_set")
        q_ready = sem("q_ready")
        q_evac = sem("q_evac")
        null_ready = sem("null_ready")
        null_evac = sem("null_evac")
        null_tr = sem("null_tr")
        m_init = sem("m_init")
        o_init = sem("o_init")
        bias_in = sem("bias_in")
        bias_masked = sem("bias_masked")
        placed = sem("placed")
        k_ready = sem("k_ready")
        k_evac = sem("k_evac")
        vt_ready = sem("vt_ready")
        vt_evac = sem("vt_evac")
        v_ready = sem("v_ready")
        v_evac = sem("v_evac")
        s_ready = sem("s_ready")
        s_added = sem("s_added")
        s_max = sem("s_max")
        m_delta = sem("m_delta")
        m_new = sem("m_new")
        m_step = sem("m_step")
        alpha_done = sem("alpha_done")
        p_done = sem("p_done")
        pt_ready = sem("pt_ready")
        pt_evac = sem("pt_evac")
        pv_ready = sem("pv_ready")
        o_scaled = sem("o_scaled")
        o_added = sem("o_added")
        rl_done = sem("rl_done")
        on_done = sem("on_done")
        ot_ready = sem("ot_ready")
        ot_evac = sem("ot_evac")
        wo_ready = sem("wo_ready")
        ln_stat = sem("ln_stat")
        ln_mv = sem("ln_mv")
        ln_rstd = sem("ln_rstd")
        ln_eps = sem("ln_eps")
        ln_norm = sem("ln_norm")
        row_done = sem("row_done")
        row_out = sem("row_out")
        passed = sem("passed")

        block = ctx.enter_context(nc.Block())

        UNIT_IN = [0] * NSH + [1 + e // 2 for e in range(E)]
        def tile_of(c):
            return (c + QT - 1) & (QT - 1)

        def chunk_of(tile):
            return (tile + 1) & (QT - 1)

        OC_M = 2
        TOT = NB * NU
        assert NG == 4 and NB == 4
        TURN_AT, PROJECT_AT = {8: 0, 11: 1, 14: 2}, {11: 0, 14: 1}
        NORMALISE_AT, FINISH_AT = {5: 0, 9: 1, 13: 2}, {13: 0}
        AHEAD = 2 * NG

        primed = (s_added, pt_ready, wo_ready, alpha_done, o_added, on_done, ln_norm, v_evac, pt_evac, row_out,
                  ob_out)

        def rows_of_tiles(eng, live, row):
            with eng.If(live > 0):
                row(0, QT - 1)
            with eng.If((live & ((1 << (QT - 1)) - 1)) > 0):
                with eng.Fori(1, QT) as t:
                    q = ((QT - 1) - t).with_bounds(min_val=0, max_val=QT - 2)
                    with eng.If((live & ((2 << q) - 1)) > 0):
                        row(t, q)

        def visible_tiles(eng, live, q, job):
            with eng.If(((live >> q) & 1) > 0):
                job(q, True)
            with eng.If((live & ((1 << q) - 1)) > 0):
                with eng.Fori(1, q + 1) as back:
                    k = (q - back).with_bounds(min_val=0, max_val=QT - 2)
                    with eng.If(((live >> k) & 1) > 0):
                        job(k, False)

        def lowest_live(live, k):
            return (live & ((1 << k) - 1)) < 1

        def wait_apart(eng, semaphore, value):
            eng.wait_ge(semaphore, value)
            eng.sem_inc(passed, 1)

        def split3(mm, acc, wa, wb_, ra, rb, first, last):
            mm(acc, wa, ra, start=first, stop=False)
            mm(acc, wa, rb, start=False, stop=False)
            return mm(acc, wb_, ra, start=False, stop=last)

        @block.sync
        def _(sp):
            for semaphore in primed:
                sp.sem_inc(semaphore, 1)
            for c in range(NC):
                sp.dma_start(xtok[:, c * NB:(c + 1) * NB, :], x_t[tile_of(c)]).then_inc(x_in[c], 16)
            for kind, src in ((0, sw_gate), (1, sw_up)):
                for u in range(NSH):
                    sp.dma_start(wraw_u[:, u, kind, :].rearrange("p (k m) -> p k m", k=KB),
                                 src.rearrange("(k p) (u m) -> u p k m", p=P, u=NSH)[u]).then_inc(w_in[0], 16)
            sp.dma_start(wraw_u[:, 0:NSH, 2, :], sw_down.rearrange("(u p) h -> p u h", p=P)).then_inc(w_in[0], 16)
            for i in range(E // 2):
                for e in (2 * i, 2 * i + 1):
                    for kind, src in ((0, w_gate), (1, w_up)):
                        sp.dma_start(wraw_u[:, NSH + e, kind, :].rearrange("p (k m) -> p k m", k=KB),
                                     src[e].rearrange("(k p) m -> p k m", p=P)).then_inc(w_in[1 + i], 16)
                    sp.dma_start(wraw_u[:, NSH + e, 2, :], w_down[e]).then_inc(w_in[1 + i], 16)
            sp.dma_start(wo[:, :, :], w_o.rearrange("(j p) h -> p j h", p=P)).then_inc(wo_in, 16)
            sp.dma_start(masku[:, :], mask.rearrange("b s -> (b s)").partition_broadcast(P)).then_inc(mask_in, 16)
            sp.dma_start(gin[:, :], g_in.rearrange("(k p) -> p k", p=P),
                          allow_slow_non_contiguous=True).then_inc(vec_in, 16)
            sp.dma_start(gout[:, :], g_out.partition_broadcast(P)).then_inc(vec_in, 16)
            sp.dma_start(nbias[:, :], null_bias.partition_broadcast(P)).then_inc(vec_in, 16)
            sp.dma_start(nv1[:, 0:DH], cond[1].partition_broadcast(P)).then_inc(vec_in, 16)
            sp.dma_start(nkb[:, :], cond[0].partition_broadcast(P)).then_inc(vec_in, 16)
            sp.wait_ge(wh_done, NU)
            sp.wait_ge(wl_done, NU)
            sp.dma_start(wq_raw, w_q.rearrange("(k p) n -> p k n", p=P)).then_inc(wq_in, 16)
            kvr = w_kv.rearrange("(k p) n -> p k n", p=P)
            sp.dma_start(wkv_raw[:, :, 0:DH], kvr[:, :, DH:2 * DH]).then_inc(wq_in, 16)
            sp.dma_start(wkv_raw[:, :, DH:2 * DH], kvr[:, :, 0:DH]).then_inc(wq_in, 16)
            sp.dma_start(wkv_raw[:, :, 2 * DH:3 * DH], kvr[:, :, 0:DH]).then_inc(wq_in, 16)

            sp.wait_ge(live_done, 1)
            live = sp.value_load(livei[0:1, 0:1], min_val=0, max_val=2 ** QT - 1)
            jobs = sp.alloc_register("sp_jobs")
            sp.reg_mov(jobs, 0)

            def row(t, q):
                def job(k, diagonal):
                    j = sp.snap(jobs, min_val=0, max_val=QT * QT)
                    sp.wait_ge(s_added, 1 + j * NW)
                    sp.dma_start(bias, fside[:, bass.ds(q * P, P), bass.ds(k * P, P)]
                                 .rearrange("h p k -> p h k")).then_inc(bias_in, 16)
                    sp.reg_add(jobs, jobs, 1)

                visible_tiles(sp, live, q, job)
                sp.wait_ge(ob_out, 1 + 16 * NC)
                for b in range(NB):
                    sp.wait_ge(row_done, t * NB + b + 1)
                    sp.dma_start(out_t[bass.ds(q, 1), :, b, :].rearrange("a p h -> p a h"),
                                 obuf[:, b:b + 1, :]).then_inc(row_out, 16)
                wait_apart(sp, row_out, 1 + t * (16 * NB) + 16 * NB)

            rows_of_tiles(sp, live, row)
            sp.wait_ge(ob_out, 1 + 16 * NC)

        @block.gpsimd
        def _(pool):
            def link(ins, n=[0]):
                n[0] += 1
                ins.then_inc(pool_chain, 1)
                pool.wait_ge(pool_chain, n[0])

            pool.memset(ident[:, :], 0.0).then_inc(zeroed, 1)
            pool.memset(identb[:, :], 0.0).then_inc(zeroed, 1)
            pool.memset(sel[:, :, :], 0.0).then_inc(zeroed, 1)
            pool.wait_ge(zeroed, 3)
            for m in (ident, identb):
                pool.affine_select(out=m[:, :], in_=m[:, :], compare_op=ALU.not_equal, fill=1.0, base=0,
                                   pattern=[[-1, P]], channel_multiplier=1).then_inc(consts, 1)
            for k in range(3):
                link(pool.affine_select(out=sel[:, :, :], in_=sel[:, :, :], compare_op=ALU.not_equal, fill=1.0,
                                        base=-k * E, pattern=[[-1, E], [0, P]], channel_multiplier=1))
            for e in range(E):
                link(pool.memset(desc[:, :, e:e + 1], float(E - e)))
            for k in range(QT):
                link(pool.memset(pow2[:, k:k + 1], float(2 ** k)))
            pool.memset(half[:, :], -0.5).then_inc(consts, 1)

            def low_part(u):
                pool.wait_ge(wh_done, u + 1)
                pool.tensor_tensor(wl[:, u, :, :], wraw_u[:, u, :, :], wh[:, u, :, :].bitcast(F32), ALU.subtract)\
                    .then_inc(wl_done, 1)

            for u in range(NU):
                low_part(u)
            pool.wait_ge(mask_in, 16)
            pool.tensor_scalar(maskb[:, :], masku[:, :], -1.0, BIG, ALU.add, ALU.mult).then_inc(mask_done, 1)
            pool.wait_ge(wo_in, 16)
            pool.wait_ge(xt_low, NC)
            pool.wait_ge(lt_ready, NC)
            link(pool.tensor_tensor(wo_sums[:, 0:4, :], wo[:, 0:4, :], wo[:, 4:8, :], ALU.add))
            link(pool.tensor_tensor(wo_sums[:, 0:2, :], wo_sums[:, 0:2, :], wo_sums[:, 2:4, :], ALU.add))
            pool.tensor_tensor(wo_sum[:, :], wo_sums[:, 0, :], wo_sums[:, 1, :], ALU.add).then_inc(wo_summed, 1)
            pool.wait_ge(wo_summed, 1)
            pool.wait_ge(vec_in, 80)
            pool.wait_ge(wq_in, 64)
            pool.tensor_tensor(wn_products, wq_raw.rearrange("p k (h d) -> p (k h) d", d=DH),
                               nkb[:, :].unsqueeze(1).to_broadcast([P, KB * NH, DH]), ALU.mult)\
                .then_inc(wn_multiplied, 1)
            pool.wait_ge(wn_multiplied, 1)
            width = DH // 2
            while width > 1:
                link(pool.tensor_tensor(wn_products[:, :, 0:width], wn_products[:, :, 0:width],
                                        wn_products[:, :, width:2 * width], ALU.add))
                width //= 2
            pool.tensor_tensor(wnf[:, :, :].rearrange("p k h -> p (k h)"), wn_products[:, :, 0],
                               wn_products[:, :, 1], ALU.add).then_inc(wn_summed, 1)
            pool.wait_ge(wn_summed, 1)
            pool.tensor_copy(wnh[:, :, :], wnf[:, :, :]).then_inc(wn_done, 1)
            pool.wait_ge(wn_done, 1)
            pool.tensor_tensor(wnl[:, :, :], wnf[:, :, :], wnh[:, :, :].bitcast(F32), ALU.subtract)\
                .then_inc(wn_done, 1)

            def after(b):
                wait_apart(pool, mv_done, (b + 1) * QT)
                pool.tensor_scalar(rstd[:, :], mv[:, :, 1], EPS, None, ALU.add).then_inc(ln_eps, 1)
                pool.wait_ge(ln_eps, b + 1)
                pool.tensor_tensor(rstd[:, :], rstd[:, :], half[:, :], ALU.pow).then_inc(rstd_done, 1)
                pool.wait_ge(oc_done, 1)
                pool.wait_ge(ob_out, 1 + b * 16)
                pool.tensor_tensor(obuf[:, :, :], xtok[:, bass.ds(b * QT, QT), :],
                                   oc[:, :].unsqueeze(1).to_broadcast([P, QT, H]), ALU.add).then_inc(ob_ready, 1)

            pool.wait_ge(oc_mv, 1)
            link(pool.tensor_scalar(rstd[:, 0:1], mv[:, 0, 1:2], EPS, None, ALU.add))
            link(pool.tensor_tensor(rstd[:, 0:1], rstd[:, 0:1], half[:, 0:1], ALU.pow))
            link(pool.tensor_scalar(oc[:, :], oc[:, :], mv[:, 0, 0:1], rstd[:, 0:1], ALU.subtract, ALU.mult))
            pool.tensor_tensor(oc[:, :], oc[:, :], gout[:, :], ALU.mult).then_inc(oc_done, 1)

            pool.wait_ge(wqh_done, 2)
            pool.tensor_tensor(wql[:, :, :], wq_raw, wqh[:, :, :].bitcast(F32), ALU.subtract).then_inc(wql_done, 1)
            pool.tensor_tensor(wkvl[:, :, :], wkv_raw, wkvh[:, :, :].bitcast(F32), ALU.subtract).then_inc(wql_done, 1)
            with pool.Fori(0, NC - 1) as c:
                after(c)
            pool.wait_ge(down_done, CREDIT + TOT)
            pool.memset(kz[:, :, :, :], 0.0).then_inc(tiles_set, 1)
            pool.memset(v1[:, :, DH:D1], 1.0).then_inc(tiles_set, 1)
            after(NC - 1)
            pool.wait_ge(live_done, 1)
            live = pool.value_load(livei[0:1, 0:1], min_val=0, max_val=2 ** QT - 1)
            jobs = pool.alloc_register("pool_jobs")
            pool.reg_mov(jobs, 0)

            def row(t, q):
                def job(k, diagonal):
                    j = pool.snap(jobs, min_val=0, max_val=QT * QT)
                    wait_apart(pool, bias_in, j * 16 + 16)
                    if diagonal:
                        pool.affine_select(out=bias, in_=bias, compare_op=ALU.is_ge, fill=-BIG, base=0,
                                           pattern=[[0, NH], [-1, P]], channel_multiplier=1).then_inc(bias_masked, 1)
                    else:
                        pool.sem_inc(bias_masked, 1)
                    pool.wait_ge(bias_masked, j + 1)
                    pool.wait_ge(mask_done, 1)

                    def place(w):
                        b, g = w // NG, w % NG
                        if w >= AHEAD:
                            wait_apart(pool, pt_ready, 1 + j * NW + w - AHEAD + 1)
                        elif w == 0:
                            pool.wait_ge(pt_ready, 1 + j * NW)
                        elif w == NG:
                            wait_apart(pool, m_init, t + 1)
                        hs = slice(g * HG, (g + 1) * HG)
                        pool.tensor_tensor(ssb[:, b % 2, hs, :], bias[:, hs, :],
                                           mask_q[:, b:b + 1, bass.ds(k * P, P)].to_broadcast([P, HG, P]),
                                           ALU.add).then_inc(placed, 1)

                    def rescale(b):
                        pool.wait_ge(alpha_done, 1 + j * NB + b + 1)
                        pool.wait_ge(o_added, 1 + j * NW)
                        pool.wait_ge(o_init, (t + 1) * NB)
                        pool.tensor_tensor(ost[:, b, :, :], ost[:, b, :, :],
                                           alpha[:, b % 2, :].unsqueeze(2).to_broadcast([P, NH, D1]),
                                           ALU.mult).then_inc(o_scaled, 1)

                    for w in range(AHEAD):
                        place(w)
                    for w in range(NW):
                        if w % NG == 0:
                            rescale(w // NG)
                        if w + AHEAD < NW:
                            place(w + AHEAD)
                    with pool.If(lowest_live(live, k)):
                        for b in range(NB):
                            wait_apart(pool, ln_mv, t * NB + b + 1)
                            pool.tensor_scalar(rstd[:, b:b + 1], mv[:, b, 1:2], EPS, None, ALU.add)\
                                .then_inc(ln_eps, 1)
                            pool.wait_ge(ln_eps, NB + t * NB + b + 1)
                            pool.tensor_tensor(rstd[:, b:b + 1], rstd[:, b:b + 1], half[:, 0:1], ALU.pow)\
                                .then_inc(ln_rstd, 1)
                    pool.reg_add(jobs, jobs, 1)

                visible_tiles(pool, live, q, job)

            rows_of_tiles(pool, live, row)

        @block.scalar
        def _(act):
            act.dma_start(small[:, 0:H], wt).then_inc(small_in, 16)
            act.dma_start(small[:, H:H + G], wg).then_inc(small_in, 16)
            act.dma_start(small[0:NB, H + P:H + P + G], cond).then_inc(small_in, 16)
            act.dma_start(small[0:NB, H + P + G:H + P + 2 * G], cond).then_inc(small_in, 16)
            act.sem_inc(g_free, CREDIT)
            act.sem_inc(y_free, CREDIT)

            def weight_high(u):
                act.wait_ge(w_in[UNIT_IN[u]], 16 * (5 if u < NSH else 6))
                act.activation(wh[:, u, :, :], wraw_u[:, u, :, :], ACT.Copy).then_inc(wh_done, 1)

            for c in range(NC):
                for k in range(KB):
                    act.wait_ge(xt_tr, KB * c + k + 1)
                    if c >= 2 and k == 0:
                        act.wait_ge(lt_ready, c - 1)
                        act.wait_ge(xt_low, c - 1)
                    act.activation(xtf[:, c % 2, k, :], bank[2 * (c % 2) + k][:, :], ACT.Copy).then_inc(xt_ev, 1)
                weight_high(c)
            act.wait_ge(dve_chain, CENTRED)
            act.activation(rt[0][:, :, :], rt[1][:, :, :], ACT.Exp, scale=0.5).then_inc(routed, 1)

            def unit_high(b, s):
                n = b * NU + s
                act.wait_ge(u_free, n + 1 + CREDIT)
                act.wait_ge(down_done, n + 1)
                act.activation(huh[:, s % 2, :], hid[:, s % 2, :], ACT.Copy).then_inc(huh_done, 1)

            def xn_evac(b, k):
                act.wait_ge(vec_in, 80)
                act.wait_ge(m_ready, b * 4 + 3 + k)
                act.activation(yt[:, k, :], misc_ps[:, :], ACT.Copy, scale=gin[:, k:k + 1]).then_inc(m_free, 1)


            def sum_evac(b):
                act.wait_ge(down_done, CREDIT + (b + 1) * NU)
                act.wait_ge(xnl_done, b * 2)
                for k in range(KB):
                    act.activation(yt[:, k, :], y_ps[k][:, :], ACT.Copy).then_inc(y_free, 1)

            def store(b):
                act.wait_ge(ob_ready, b + 1)
                act.dma_start(out_t[bass.ds(tile_of(b), 1)].rearrange("a p b h -> p (a b) h"), obuf[:, :, :])\
                    .then_inc(ob_out, 16)

            def experts(b, first):
                for s in range(NU):
                    if s >= 1:
                        unit_high(b, s - 1)
                    elif not first:
                        unit_high(b - 1, NU - 1)
                    act.wait_ge(g_ready, b * NU + s + 1)
                    act.wait_ge(hul_done, b * NU + s + 1)
                    act.activation(hid[:, s % 2, :], gate_ps[s % 2][:, :], ACT.Copy).then_inc(g_free, 1)
                    if first and s + NC < NU:
                        weight_high(s + NC)
                    if first and s == NU - 2:
                        act.wait_ge(wq_in, 64)
                        act.activation(wqh[:, :, :], wq_raw, ACT.Copy).then_inc(wqh_done, 1)
                        act.activation(wkvh[:, :, :], wkv_raw, ACT.Copy).then_inc(wqh_done, 1)
                    if not first:
                        if s == 0:
                            act.wait_ge(wn_summed, 1)
                            sum_evac(b - 1)
                        if s in (6, 7):
                            xn_evac(b - 1, s - 6)
                        if s == 8:
                            store(b - 1)

            experts(0, True)
            with act.Fori(1, NC) as b:
                experts(b, False)
            unit_high(NC - 1, NU - 1)
            sum_evac(NC - 1)

            def null_evacuate(t):
                if not isinstance(t, int):
                    act.wait_ge(wo_ready, 1 + t * NB)
                act.wait_ge(null_ready, t + 1)
                act.activation(null_t, proj_ps[0][0:NH, :].rearrange("h (b t) -> h b t", b=NB), ACT.Copy,
                               scale=float(DH) ** -0.5).then_inc(null_evac, 1)

            def q_evacuate(t, j):
                act.wait_ge(q_ready, t * PAIRS + j + 1)
                act.activation(qt_sb[:, j, :, :].rearrange("p b t -> p (b t)"), logit_ps[j % 2][:, :], ACT.Copy,
                               scale=float(DH) ** -0.5).then_inc(q_evac, 1)

            def start_output(t, b):
                if b == 0 and not isinstance(t, int):
                    act.wait_ge(on_done, 1 + t * NB)
                act.activation(ost[:, b, :, :], nv1[:, :].unsqueeze(1).to_broadcast([P, NH, D1]), ACT.Copy)\
                    .then_inc(o_init, 1)

            null_evacuate(0)
            for j in range(PAIRS):
                if j == PAIRS - 1:
                    xn_evac(NC - 1, 0)
                q_evacuate(0, j)
                if 1 <= j < 1 + NB:
                    start_output(0, j - 1)
            xn_evac(NC - 1, 1)
            store(NC - 1)

            act.wait_ge(live_done, 1)
            live = act.value_load(livei[0:1, 0:1], min_val=0, max_val=2 ** QT - 1)
            jobs = act.alloc_register("act_jobs")
            act.reg_mov(jobs, 0)

            def row(t, q):
                if not isinstance(t, int):
                    null_evacuate(t)
                    for j in range(PAIRS):
                        q_evacuate(t, j)
                        if j < NB:
                            start_output(t, j)

                def job(k, diagonal):
                    j = act.snap(jobs, min_val=0, max_val=QT * QT)
                    act.wait_ge(k_ready, j + 1)
                    act.wait_ge(tiles_set, 2)
                    act.activation(kz[0:DH, :, 0, :], pt_ps[0][0:DH, :].rearrange("p (b t) -> p b t", b=NB),
                                   ACT.Copy).then_inc(k_evac, 1)
                    act.activation(kz[DH:P, :, 1, :], pt_ps[0][DH:P, :].rearrange("p (b t) -> p b t", b=NB),
                                   ACT.Copy).then_inc(k_evac, 1)
                    act.wait_ge(vt_ready, j + 1)
                    act.activation(vt[:, :, :].rearrange("p b t -> p (b t)"), pt_ps[1][0:DH, :],
                                   ACT.Copy).then_inc(vt_evac, 1)
                    act.wait_ge(v_ready, j + 1)
                    act.activation(v1[:, :, 0:DH], pt_ps[0][:, 0:NB * DH]
                                   .rearrange("p (b d) -> p b d", b=NB), ACT.Copy).then_inc(v_evac, 1)

                    def probs(w):
                        b, g = w // NG, w % NG
                        act.wait_ge(m_new, j * NB + b + 1)
                        if g == 0:
                            act.activation(alpha[:, b % 2, :], dm[:, b % 2, :], ACT.Exp)\
                                .then_inc(alpha_done, 1)
                        for h in range(g * HG, (g + 1) * HG):
                            ins = act.activation(ssb[:, b % 2, h, :], ssb[:, b % 2, h, :], ACT.Exp,
                                                 bias=mneg[:, b, h:h + 1])
                        ins.then_inc(p_done, 1)

                    def transposed(w):
                        act.wait_ge(pt_ready, 1 + j * NW + w + 1)
                        act.activation(pt[:, w % 2, :, :].rearrange("p h t -> p (h t)"),
                                       pt_ps[w % 2][:, :], ACT.Copy).then_inc(pt_evac, 1)

                    for w in range(NG // 2):
                        probs(w)
                    def output_transposed(b):
                        for i in range(2):
                            act.wait_ge(ot_ready, t * (2 * NB) + 2 * b + i + 1)
                            act.activation(on_t[b % 2][:, i, :], s_ps[i][:, :], ACT.Copy).then_inc(ot_evac, 1)

                    for w in range(NW):
                        transposed(w)
                        if w in TURN_AT:
                            with act.If(lowest_live(live, k)):
                                output_transposed(TURN_AT[w])
                        if w + NG // 2 < NW:
                            probs(w + NG // 2)
                    with act.If(lowest_live(live, k)):
                        output_transposed(NB - 1)
                    act.reg_add(jobs, jobs, 1)

                visible_tiles(act, live, q, job)

            rows_of_tiles(act, live, row)

        @block.vector
        def _(dve):
            chain = [0]

            def link(ins):
                chain[0] += 1
                ins.then_inc(dve_chain, 1)
                dve.wait_ge(dve_chain, chain[0])

            dve.sem_inc(u_free, CREDIT)
            dve.sem_inc(hul_done, CREDIT)
            dve.sem_inc(wb_free, 1)
            dve.wait_ge(small_tr, 1)
            link(dve.tensor_copy(wtT[:, :, :].rearrange("p k e -> p (k e)"), misc_ps[:, 0:KB * 8]))
            link(dve.tensor_copy(wgT[:, :], misc_ps[0:G, 16:24]))
            link(dve.tensor_copy(condT[:, :], misc_ps[:, 24:28]))
            link(dve.tensor_copy(nvc[:, :], condT[:, 1:2].to_broadcast([P, P])))
            dve.memset(nv1[:, DH:D1], 1.0).then_inc(small_ev, 1)

            def x_high(c):
                dve.wait_ge(xt_ev, KB * (c + 1))
                dve.tensor_copy(xth[:, :, c * S:(c + 1) * S], xtf[:, c % 2, :, :]).then_inc(xt_high, 1)

            def x_low(c):
                dve.wait_ge(xt_high, c + 1)
                cols = slice(c * S, (c + 1) * S)
                dve.tensor_tensor(xtl[:, :, cols], xtf[:, c % 2, :, :], xth[:, :, cols].bitcast(F32),
                                  ALU.subtract).then_inc(xt_low, 1)

            def add_batch_logits(c):
                dve.wait_ge(lt_ready, c + 1)
                if c >= 2:
                    dve.wait_ge(routed, c - 1)
                dve.tensor_tensor(logit_t[:, c % 2, :].rearrange("e (b t) -> e b t", b=NB),
                                  y_ps[c % 2][0:E, :].rearrange("e (b t) -> e b t", b=NB),
                                  glog[:, :].unsqueeze(2).to_broadcast([E, NB, P]), ALU.add).then_inc(lt_evac, 1)

            x_high(0)
            x_low(0)
            dve.wait_ge(glog_ready, 1)
            link(dve.tensor_copy(glog[:, :], misc_ps[0:E, 32:32 + NB]))
            add_batch_logits(0)
            x_high(1)
            x_low(1)
            for c in range(1, NC):
                add_batch_logits(c)

            full = [P, NT, E]
            e_, c_, k_, o_ = rt
            dve.wait_ge(routed, NC)
            logits = wb_ps[:, 0:NT * E].rearrange("p (t e) -> p t e", e=E)
            link(dve.reduce_max(r1[0][:, :, 0], logits, AX_X))
            link(dve.tensor_tensor(c_[:, :, :], logits, r1[0][:, :, :].to_broadcast(full), ALU.subtract))
            assert chain[0] == CENTRED, chain[0]

            def first_place(hot):
                link(dve.reduce_max(r1[3][:, :, 0], k_[:, :, :], AX_X))
                link(dve.tensor_tensor(hot[:, :, :], k_[:, :, :], r1[3][:, :, :].to_broadcast(full), ALU.is_equal))

            def first_choice():
                dve.wait_ge(consts, 3)
                link(dve.scalar_tensor_tensor(out=k_[:, :, :], in0=c_[:, :, :], scalar=0.0, in1=desc[:, :, :],
                                              op0=ALU.is_equal, op1=ALU.mult))
                first_place(o_)

            def second_choice():
                dve.wait_ge(routed, NC + 1)
                link(dve.scalar_tensor_tensor(out=c_[:, :, :], in0=o_[:, :, :], scalar=-BIG, in1=c_[:, :, :],
                                              op0=ALU.mult, op1=ALU.add))
                link(dve.reduce_max(r1[1][:, :, 0], c_[:, :, :], AX_X))
                link(dve.tensor_tensor(k_[:, :, :], c_[:, :, :], r1[1][:, :, :].to_broadcast(full), ALU.is_equal))
                link(dve.tensor_tensor(k_[:, :, :], k_[:, :, :], desc[:, :, :], ALU.mult))
                first_place(c_)

            def routing_weights():
                link(dve.reduce_sum(r1[0][:, :, 0], e_[:, :, :], AX_X))
                link(dve.tensor_tensor(o_[:, :, :], o_[:, :, :], c_[:, :, :], ALU.add))
                link(dve.tensor_tensor(e_[:, :, :], e_[:, :, :], o_[:, :, :], ALU.mult))
                link(dve.reduce_sum(r1[1][:, :, 0], e_[:, :, :], AX_X))
                link(dve.scalar_tensor_tensor(out=r1[1][:, :, :], in0=r1[0][:, :, :], scalar=1e-20,
                                              in1=r1[1][:, :, :], op0=ALU.mult, op1=ALU.add))
                link(dve.reciprocal(r1[1][:, :, :], r1[1][:, :, :]))
                link(dve.tensor_tensor(e_[:, :, :], e_[:, :, :], r1[1][:, :, :].to_broadcast(full), ALU.mult))
                link(dve.tensor_copy(w3[:, :, 0, :], e_[:, :, :]))
                link(dve.tensor_tensor(c_[:, :, :], e_[:, :, :], w3[:, :, 0, :], ALU.subtract))
                link(dve.tensor_copy(w3[:, :, 1, :], c_[:, :, :]))
                link(dve.tensor_tensor(e_[:, :, :], c_[:, :, :], w3[:, :, 1, :], ALU.subtract))
                dve.tensor_copy(w3[:, :, 2, :], e_[:, :, :]).then_inc(w3_ready, 1)

            def weights_kept():
                dve.wait_ge(w3_tr, 1)
                dve.tensor_copy(w3t[:, 0:NT * P // 2], wb_ps[0:3 * E, :].bitcast(BF16)).then_inc(w3_ev, 1)
                dve.wait_ge(w3_tr, 2)
                dve.tensor_copy(w3t[:, NT * P // 2:NT * P], misc_ps[0:3 * E, :].bitcast(BF16)).then_inc(m_free, 1)

            def tile_seen(k):
                dve.wait_ge(mask_in, 16)
                link(dve.tensor_reduce(live4[:, k:k + 1], masku[0:1, :].rearrange("o (b k s) -> o k b s", b=NB, k=QT)
                                       [:, k], AX_XY, ALU.max))

            def live_word():
                link(dve.tensor_tensor(live4[:, :], live4[:, :], pow2[:, :], ALU.mult))
                link(dve.reduce_sum(livew[:, :], live4[:, :], AX_X))
                dve.tensor_copy(livei[:, :], livew[:, :]).then_inc(live_done, 1)

            def unit_low(b, s):
                dve.wait_ge(huh_done, b * NU + s + 1)
                dve.tensor_tensor(hul[:, s % 2, :], hid[:, s % 2, :], huh[:, s % 2, :].bitcast(F32), ALU.subtract)\
                    .then_inc(hul_done, 1)

            def null_row():
                dve.wait_ge(oc_ready, 1)
                dve.tensor_copy(oc[:, :], misc_ps[:, 0:H]).then_inc(m_free, 1)
                dve.wait_ge(m_free, 2)
                dve.bn_stats(st6[:, 0, :], oc[:, :]).then_inc(oc_stat, 1)
                dve.wait_ge(oc_stat, 1)
                dve.bn_aggr(mv[:, 0, :], st6[:, 0, :]).then_inc(oc_mv, 1)

            def add_moe(b, i):
                dve.wait_ge(m_ready, b * 4 + 1 + i)
                rows = xtok[:, bass.ds(b * QT + 2 * i, 2), :]
                dve.tensor_tensor(rows, rows, misc_ps[:, :].rearrange("p (t h) -> p t h", t=2), ALU.add)\
                    .then_inc(m_free, 1)

            def stats(b):
                dve.wait_ge(oc_done, 1)
                wait_apart(dve, m_free, OC_M + b * 4 + 2)
                for t in range(QT):
                    dve.bn_stats(st6[:, t, :], xtok[:, bass.ds(b * QT + t, 1), :]
                                 .rearrange("p a h -> p (a h)")).then_inc(st_done, 1)
                wait_apart(dve, st_done, (b + 1) * QT)
                for t in range(QT):
                    dve.bn_aggr(mv[:, t, :], st6[:, t, :]).then_inc(mv_done, 1)

            def normalise(b):
                dve.wait_ge(rstd_done, b + 1)
                for t in range(QT):
                    dve.tensor_scalar(xn[:, t, :], xtok[:, bass.ds(b * QT + t, 1), :].rearrange("p a h -> p (a h)"),
                                      mv[:, t, 0:1], rstd[:, t:t + 1], ALU.subtract, ALU.mult).then_inc(xn_done, 1)

            def split_xn(b, k):
                dve.wait_ge(m_free, OC_M + b * 4 + 3 + k)
                dst = xth[:, k, bass.ds(b * S, S)]
                dve.tensor_copy(dst, yt[:, k, :]).then_inc(xnh_done, 1)
                dve.wait_ge(xnh_done, b * 2 + k + 1)
                dve.tensor_tensor(xtl[:, k, bass.ds(b * S, S)], yt[:, k, :], dst.bitcast(F32), ALU.subtract)\
                    .then_inc(xnl_done, 1)

            first_choice()

            def experts(b, first):
                for s in range(NU):
                    n = b * NU + s
                    if s >= 1:
                        unit_low(b, s - 1)
                    elif not first:
                        unit_low(b - 1, NU - 1)
                    if first and s == 1:
                        second_choice()
                    if first and s == NSH:
                        routing_weights()
                        weights_kept()
                    dve.wait_ge(g_free, n + 1 + CREDIT)
                    dve.scalar_tensor_tensor(out=hid[:, s % 2, :], in0=hid[:, s % 2, :], scalar=LEAK,
                                             in1=hid[:, s % 2, :], op0=ALU.mult, op1=ALU.max).then_inc(leaked, 1)
                    dve.wait_ge(leaked, n + 1)
                    if s >= NSH:
                        r = b * E + s - NSH
                        dve.wait_ge(wb_ready, r + 1)
                        dve.tensor_tensor(hid[:, s % 2, :], hid[:, s % 2, :], wb_ps[:, :], ALU.mult)\
                            .then_inc(wb_free, 1)
                        dve.wait_ge(wb_free, r + 2)
                    dve.wait_ge(u_ready, n + 1)
                    dve.tensor_tensor(hid[:, s % 2, :], hid[:, s % 2, :], up_ps[s % 2][:, :], ALU.mult)\
                        .then_inc(u_free, 1)
                    if first and s in (3, 5):
                        x_high(2 + (s - 3) // 2)
                    if first and s in (4, 6):
                        x_low(2 + (s - 4) // 2)
                    if first and s in (7, 8):
                        tile_seen(2 * (s - 7))
                        tile_seen(2 * (s - 7) + 1)
                    if first and s == NU - 1:
                        live_word()
                    if first and s == NU - 1:
                        null_row()
                    if not first:
                        if s in (2, 3):
                            add_moe(b - 1, s - 2)
                        if s == 4:
                            stats(b - 1)
                        if s == 5:
                            normalise(b - 1)
                        if s in (6, 7):
                            split_xn(b - 1, s - 6)

            experts(0, True)
            with dve.Fori(1, NC) as b:
                experts(b, False)
            unit_low(NC - 1, NU - 1)
            for i in range(2):
                add_moe(NC - 1, i)
            stats(NC - 1)
            normalise(NC - 1)
            for k in range(KB):
                split_xn(NC - 1, k)

            live = dve.value_load(livei[0:1, 0:1], min_val=0, max_val=2 ** QT - 1)
            jobs = dve.alloc_register("dve_jobs")
            dve.reg_mov(jobs, 0)

            def row(t, q):
                dve.wait_ge(null_tr, t + 1)
                dve.scalar_tensor_tensor(out=mneg[:, :, :], scalar=-1.0,
                                         in0=proj_ps[0][:, 0:NB * NH].rearrange("p (b h) -> p b h", b=NB),
                                         in1=nbias[:, :].unsqueeze(1).to_broadcast([P, NB, NH]),
                                         op0=ALU.mult, op1=ALU.subtract).then_inc(m_init, 1)

                def job(k, diagonal):
                    j = dve.snap(jobs, min_val=0, max_val=QT * QT)

                    def add_bias(w):
                        b, g = w // NG, w % NG
                        dve.wait_ge(s_ready, j * NW + w + 1)
                        dve.wait_ge(placed, j * NW + w + 1)
                        hs = slice(g * HG, (g + 1) * HG)
                        dve.tensor_tensor(ssb[:, b % 2, hs, :],
                                          s_ps[g][:, :].rearrange("p (h k) -> p h k", h=HG),
                                          ssb[:, b % 2, hs, :], ALU.add).then_inc(s_added, 1)
                        if g == 0 and b > 0:
                            dve.wait_ge(m_new, j * NB + b)
                        dve.wait_ge(s_added, 1 + j * NW + w + 1)
                        dve.reduce_max(mx[:, hs], ssb[:, b % 2, hs, :], AX_X).then_inc(s_max, 1)

                    def maximum(b):
                        dve.wait_ge(s_max, j * NW + (b + 1) * NG)
                        dve.wait_ge(m_init, t + 1)
                        dve.scalar_tensor_tensor(out=mx[:, :], in0=mx[:, :], scalar=-1.0, in1=mneg[:, b, :],
                                                 op0=ALU.mult, op1=ALU.min).then_inc(m_step, 1)
                        dve.wait_ge(m_step, j * NB + b + 1)
                        dve.wait_ge(alpha_done, 1 + j * NB + max(b - 1, 0))
                        dve.tensor_tensor(dm[:, b % 2, :], mx[:, :], mneg[:, b, :], ALU.subtract)\
                            .then_inc(m_delta, 1)
                        dve.wait_ge(m_delta, j * NB + b + 1)
                        dve.tensor_copy(mneg[:, b, :], mx[:, :]).then_inc(m_new, 1)

                    def gather(w):
                        b, g = w // NG, w % NG
                        dve.wait_ge(pv_ready, j * NW + w + 1)
                        if g == 0:
                            dve.wait_ge(o_scaled, j * NB + b + 1)
                        hs = slice(g * HG, (g + 1) * HG)
                        dve.tensor_tensor(ost[:, b, hs, :], ost[:, b, hs, :],
                                          pv_ps[g % 2][:, 0:HG * D1].rearrange("p (h d) -> p h d", h=HG),
                                          ALU.add).then_inc(o_added, 1)

                    for w in range(AHEAD):
                        add_bias(w)
                        if w % NG == NG - 1:
                            maximum(w // NG)
                    def normalise_output(b):
                        n = t * NB + b
                        dve.wait_ge(o_added, 1 + j * NW + (b + 1) * NG)
                        dve.reciprocal(rl[:, b, :], ost[:, b, :, DH]).then_inc(rl_done, 1)
                        if b >= 1:
                            dve.wait_ge(ot_ready, 2 * n)
                        dve.wait_ge(rl_done, n + 1)
                        dve.tensor_tensor(on, ost[:, b, :, 0:DH],
                                          rl[:, b, :].unsqueeze(2).to_broadcast([P, NH, DH]),
                                          ALU.mult).then_inc(on_done, 1)

                    def finish_rows(b):
                        n = t * NB + b
                        acc = s_ps[2 + b % 2][:, 0:H]
                        dve.wait_ge(wo_ready, 1 + n + 1)
                        dve.bn_stats(st6[:, b, :], acc).then_inc(ln_stat, 1)
                        wait_apart(dve, ln_stat, n + 1)
                        dve.bn_aggr(mv[:, b, :], st6[:, b, :]).then_inc(ln_mv, 1)
                        if b == 0:
                            dve.wait_ge(row_out, 1 + t * (16 * NB))
                            dve.wait_ge(ob_out, 1 + 16 * NC)
                        wait_apart(dve, ln_mv, n + 1)
                        dve.scalar_tensor_tensor(out=obuf[:, b, :], in0=acc, scalar=mv[:, b, 0:1],
                                                 in1=gout[:, :], op0=ALU.subtract, op1=ALU.mult)\
                            .then_inc(ln_norm, 1)
                        dve.wait_ge(ln_norm, 1 + n + 1)
                        dve.wait_ge(ln_rstd, n + 1)
                        dve.scalar_tensor_tensor(out=obuf[:, b, :], in0=obuf[:, b, :],
                                                 scalar=rstd[:, b:b + 1],
                                                 in1=xtok[:, bass.ds(chunk_of(q) * NB + b, 1), :]
                                                 .rearrange("p a h -> p (a h)"),
                                                 op0=ALU.mult, op1=ALU.add).then_inc(row_done, 1)

                    for w in range(NW):
                        if w + AHEAD < NW:
                            add_bias(w + AHEAD)
                        if w >= 1:
                            gather(w - 1)
                        if w + AHEAD < NW and w % NG == NG - 1:
                            maximum((w + AHEAD) // NG)
                        if w in NORMALISE_AT:
                            with dve.If(lowest_live(live, k)):
                                normalise_output(NORMALISE_AT[w])
                                if w in FINISH_AT:
                                    finish_rows(FINISH_AT[w])
                    gather(NW - 1)
                    with dve.If(lowest_live(live, k)):
                        normalise_output(NB - 1)
                        for b in range(1, NB):
                            finish_rows(b)
                    dve.reg_add(jobs, jobs, 1)

                visible_tiles(dve, live, q, job)

            rows_of_tiles(dve, live, row)

        @block.tensor
        def _(pe):
            mm = nc.tensor.matmul
            tr = nc.tensor.transpose
            pe.sem_inc(down_done, CREDIT)
            pe.wait_ge(consts, 2)
            pe.wait_ge(small_in, 64)
            for k in range(KB):
                tr(misc_ps[:, 8 * k:8 * k + 8], small[:, k * P:(k + 1) * P], ident[0:8, 0:8])
            tr(misc_ps[0:G, 16:24], small[:, H:H + G], ident[0:8, 0:8])
            tr(misc_ps[:, 24:28], small[0:NB, H + P:H + 2 * P], ident[0:NB, 0:NB]).then_inc(small_tr, 1)

            def x_transposes(c):
                pe.wait_ge(x_in[c], 16)
                for k in range(KB):
                    if c >= 2:
                        pe.wait_ge(xt_ev, KB * (c - 2) + k + 1)
                    for b in range(NB):
                        ins = tr(bank[2 * (c % 2) + k][:, b * P:(b + 1) * P],
                                 xtok[:, c * NB + b, k * P:(k + 1) * P], ident[:, :])
                    ins.then_inc(xt_tr, 1)

            def router(c):
                pe.wait_ge(xt_ev, KB * (c + 1))
                if c >= 2:
                    pe.wait_ge(lt_evac, c - 1)
                for k in range(KB):
                    ins = mm(y_ps[c % 2][0:E, :], wtT[:, k, :], xtf[:, c % 2, k, :],
                             start=(k == 0), stop=(k == KB - 1))
                ins.then_inc(lt_ready, 1)

            def logit_transposes(c):
                pe.wait_ge(lt_evac, c + 1)
                for b in range(NB):
                    ins = tr(wb_ps[:, (c * NB + b) * E:(c * NB + b + 1) * E],
                             logit_t[:, c % 2, b * P:(b + 1) * P], ident[0:E, 0:E])
                ins.then_inc(routed, 1)

            x_transposes(0)
            x_transposes(1)
            pe.wait_ge(small_ev, 1)
            mm(misc_ps[0:E, 32:32 + NB], wgT[:, :], condT[0:G, :], start=True, stop=True).then_inc(glog_ready, 1)
            for c in range(NC):
                router(c)
                if c >= 1:
                    logit_transposes(c - 1)
                if c + 2 < NC:
                    x_transposes(c + 2)
            logit_transposes(NC - 1)

            def weights_transposed():
                pe.wait_ge(w3_ready, 1)
                for i, dst in enumerate((wb_ps, misc_ps)):
                    view = dst[0:3 * E, :].bitcast(BF16)
                    for n in range(NT // 2):
                        ins = tr(view[:, n * P:(n + 1) * P],
                                 w3[:, i * NT // 2 + n, :, :].rearrange("p k e -> p (k e)"), identb[:, :])
                    ins.then_inc(w3_tr, 1)
                pe.wait_ge(w3_ev, 1)

            def down(b, s):
                n = b * NU + s
                pe.wait_ge(hul_done, n + 1 + CREDIT)
                if s == 0:
                    pe.wait_ge(y_free, CREDIT + b * KB)
                for k in range(KB):
                    cols = slice(k * P, (k + 1) * P)
                    ins = split3(mm, y_ps[k][:, :], wh[:, s, 2, cols], wl[:, s, 2, cols],
                                 huh[:, s % 2, :], hul[:, s % 2, :], s == 0, s == NU - 1)
                ins.then_inc(down_done, 1)

            def spread_weight(b, s):
                wait_apart(pe, wb_free, b * E + s - NSH + 1)
                mm(wb_ps[:, :], sel[:, s - NSH, :], w3t[:, bass.ds(b * S, S)], start=True, stop=True)\
                    .then_inc(wb_ready, 1)

            def null_row():
                pe.wait_ge(wo_summed, 1)
                pe.wait_ge(m_free, 1)
                mm(misc_ps[:, 0:H], nvc[:, :], wo_sum[:, :], start=True, stop=True).then_inc(oc_ready, 1)

            def moe_rows(b, i):
                pe.wait_ge(y_free, CREDIT + (b + 1) * KB)
                pe.wait_ge(m_free, OC_M + b * 4 + i)
                for t in range(2):
                    for k in range(KB):
                        ins = tr(misc_ps[:, t * H + k * P:t * H + (k + 1) * P],
                                 yt[:, k, (2 * i + t) * P:(2 * i + t + 1) * P], ident[:, :])
                ins.then_inc(m_ready, 1)

            def xn_cols(b, k):
                pe.wait_ge(xn_done, (b + 1) * QT)
                pe.wait_ge(m_free, OC_M + b * 4 + 2 + k)
                for t in range(QT):
                    ins = tr(misc_ps[:, t * P:(t + 1) * P], xn[:, t, k * P:(k + 1) * P], ident[:, :])
                ins.then_inc(m_ready, 1)

            def product(b, s, kind, acc):
                for k in range(KB):
                    cols = slice(k * M, (k + 1) * M)
                    ins = split3(mm, acc, wh[:, s, kind, cols], wl[:, s, kind, cols],
                                 xth[:, k, bass.ds(b * S, S)], xtl[:, k, bass.ds(b * S, S)], k == 0, k == KB - 1)
                return ins

            def gate(b, s):
                pe.wait_ge(g_free, b * NU + s + 1)
                product(b, s, 0, gate_ps[s % 2][:, :]).then_inc(g_ready, 1)

            def up(b, s):
                pe.wait_ge(u_free, b * NU + s + 1)
                product(b, s, 1, up_ps[s % 2][:, :]).then_inc(u_ready, 1)

            def first_units():
                pe.wait_ge(xt_low, 1)
                for s in range(NSH + 2):
                    pe.wait_ge(wl_done, s + 1)
                    gate(0, s)
                    up(0, s)
                    if 1 <= s <= NSH:
                        down(0, s - 1)
                weights_transposed()
                spread_weight(0, NSH)
                pe.wait_ge(wl_done, NSH + 3)
                gate(0, NSH + 2)
                spread_weight(0, NSH + 1)
                up(0, NSH + 2)
                down(0, NSH)
                spread_weight(0, NSH + 2)
                down(0, NSH + 1)
                return NSH + 3

            def experts(b, first):
                for s in range(first_units() if first else 0, NU):
                    if first:
                        pe.wait_ge(wl_done, s + 1)
                    gate(b, s)
                    if s >= NSH:
                        spread_weight(b, s)
                    up(b, s)
                    if s >= 1:
                        down(b, s - 1)
                    else:
                        down(b - 1, NU - 1)
                    if first and s == NU - 1:
                        pe.wait_ge(xt_low, NC)
                        null_row()
                    if not first:
                        if s in (2, 3):
                            moe_rows(b - 1, s - 2)
                        if s in (6, 7):
                            xn_cols(b - 1, s - 6)

            experts(0, True)
            with pe.Fori(1, NC) as b:
                experts(b, False)
            pe.wait_ge(live_done, 1)
            live = pe.value_load(livei[0:1, 0:1], min_val=0, max_val=2 ** QT - 1)
            jobs = pe.alloc_register("pe_jobs")
            pe.reg_mov(jobs, 0)
            down(NC - 1, NU - 1)

            def project(acc, high, low, tile):
                first_col = chunk_of(tile) * S
                for k in range(KB):
                    ins = split3(mm, acc, high(k), low(k), xth[:, k, bass.ds(first_col, S)],
                                 xtl[:, k, bass.ds(first_col, S)], k == 0, k == KB - 1)
                return ins

            def q_project(t, j):
                if isinstance(t, int) and j < 2:
                    pe.wait_ge(g_free, TOT + CREDIT)
                if j >= 2:
                    pe.wait_ge(q_evac, t * PAIRS + j - 1)
                project(logit_ps[j % 2][:, :], lambda k: wqh[:, k, j * P:(j + 1) * P],
                        lambda k: wql[:, k, j * P:(j + 1) * P], (QT - 1) - t).then_inc(q_ready, 1)

            def null_project(t):
                project(proj_ps[0][0:NH, :], lambda k: wnh[:, k, :], lambda k: wnl[:, k, :], (QT - 1) - t)\
                    .then_inc(null_ready, 1)

            def null_transposes(t):
                wait_apart(pe, null_evac, t + 1)
                for b in range(NB):
                    ins = tr(proj_ps[0][:, b * NH:(b + 1) * NH], null_t[:, b, :], ident[0:NH, 0:NH])
                ins.then_inc(null_tr, 1)

            pe.wait_ge(wql_done, 2)
            pe.wait_ge(wn_done, 2)
            pe.wait_ge(wb_free, 1 + NC * E)
            null_project(0)
            for j in range(PAIRS):
                q_project(0, j)
                if j == 0:
                    moe_rows(NC - 1, 0)
                if j == 1:
                    moe_rows(NC - 1, 1)
                if j == 3:
                    null_transposes(0)
                if j == PAIRS - 2:
                    xn_cols(NC - 1, 0)
            xn_cols(NC - 1, 1)

            pe.wait_ge(u_free, TOT + CREDIT)
            pe.wait_ge(wo_in, 16)

            def row(t, q):
                if not isinstance(t, int):
                    j = pe.snap(jobs, min_val=0, max_val=QT * QT)
                    pe.wait_ge(s_added, 1 + j * NW)
                    pe.wait_ge(ln_norm, 1 + t * NB)
                    null_project(t)
                    for j in range(PAIRS):
                        q_project(t, j)
                    null_transposes(t)
                wait_apart(pe, q_evac, (t + 1) * PAIRS)

                def job(k, diagonal):
                    j = pe.snap(jobs, min_val=0, max_val=QT * QT)
                    pe.wait_ge(pt_evac, 1 + j * NW)
                    pe.wait_ge(xnl_done, (chunk_of(k) + 1) * KB)
                    project(pt_ps[0][:, :], lambda kk: wkvh[:, kk, DH:3 * DH],
                            lambda kk: wkvl[:, kk, DH:3 * DH], k).then_inc(k_ready, 1)
                    project(pt_ps[1][:, :], lambda kk: wkvh[:, kk, 0:2 * DH],
                            lambda kk: wkvl[:, kk, 0:2 * DH], k).then_inc(vt_ready, 1)
                    wait_apart(pe, k_evac, j * 2 + 2)
                    wait_apart(pe, m_init, t + 1)

                    def logits(n):
                        b, g = n // NG, n % NG
                        w = j * NW + n
                        acc = s_ps[g]
                        wait_apart(pe, s_added, 1 + (w - NG + 1 if b > 0 else j * NW))
                        for i in range(2):
                            ins = mm(acc[:, i * 2 * P:(i + 1) * 2 * P], qt_sb[:, 2 * g + i, b, :],
                                     kz[:, b, :, :].rearrange("p a k -> p (a k)"),
                                     start=True, stop=True)
                        ins.then_inc(s_ready, 1)

                    def transposes(w):
                        b, g = w // NG, w % NG
                        pe.wait_ge(p_done, j * NW + w + 1)
                        pe.wait_ge(pt_evac, 1 + j * NW + max(w - 1, 0))
                        for i in range(HG):
                            ins = tr(pt_ps[g % 2][:, i * P:(i + 1) * P], ssb[:, b % 2, g * HG + i, :],
                                     ident[:, :])
                        ins.then_inc(pt_ready, 1)

                    def values(w):
                        b, g = w // NG, w % NG
                        pe.wait_ge(pt_evac, 1 + j * NW + w + 1)
                        pe.wait_ge(o_added, 1 + j * NW + max(w - 1, 0))
                        for i in range(HG):
                            ins = mm(pv_ps[g % 2][:, i * D1:(i + 1) * D1], pt[:, g % 2, i, :], v1[:, b, :],
                                     start=True, stop=True)
                        ins.then_inc(pv_ready, 1)

                    pe.wait_ge(m_free, OC_M + 4 * NC)
                    for w in range(NG):
                        logits(w)
                    for w in range(NG, AHEAD):
                        if w == AHEAD - 2:
                            wait_apart(pe, vt_evac, j + 1)
                            for b in range(NB):
                                ins = tr(pt_ps[0][:, b * DH:(b + 1) * DH], vt[:, b, :], ident[0:DH, 0:DH])
                            ins.then_inc(v_ready, 1)
                        logits(w)
                    wait_apart(pe, v_evac, 1 + j + 1)
                    def out_transposes(b):
                        n = t * NB + b
                        pe.wait_ge(on_done, 1 + n + 1)
                        if b == 0:
                            pe.wait_ge(s_added, 1 + (j + 1) * NW)
                        for i in range(2):
                            if b >= 1:
                                pe.wait_ge(ot_evac, 2 * (n - 1) + i + 1)
                            for c in range(4):
                                ins = tr(s_ps[i][:, c * P:(c + 1) * P],
                                         hid[:, i, c * P:(c + 1) * P], ident[:, :])
                            ins.then_inc(ot_ready, 1)

                    def out_project(b):
                        n = t * NB + b
                        pe.wait_ge(ot_evac, 2 * (n + 1))
                        if b >= 2:
                            pe.wait_ge(ln_norm, 1 + n - 1)
                        for jj in range(PAIRS):
                            ins = mm(s_ps[2 + b % 2][:, 0:H], on_t[b % 2][:, jj // 4, (jj % 4) * P:(jj % 4 + 1) * P],
                                     wo[:, jj, :], start=(jj == 0), stop=(jj == PAIRS - 1))
                        ins.then_inc(wo_ready, 1)

                    for w in range(NW):
                        transposes(w)
                        if w + AHEAD < NW:
                            logits(w + AHEAD)
                        if w >= 1:
                            values(w - 1)
                        if w in TURN_AT:
                            with pe.If(lowest_live(live, k)):
                                if w in PROJECT_AT:
                                    out_project(PROJECT_AT[w])
                                out_transposes(TURN_AT[w])
                    values(NW - 1)
                    with pe.If(lowest_live(live, k)):
                        out_project(NB - 2)
                        out_transposes(NB - 1)
                        out_project(NB - 1)
                    pe.reg_add(jobs, jobs, 1)

                visible_tiles(pe, live, q, job)

            rows_of_tiles(pe, live, row)


CENTRED = 7


_INS = ["x", "cond_64", "fside_16xSxS_0", "mask_BxS_bk0", "L0_cond_wt", "L0_cond_wg", "L0_cond_w_gate",
        "L0_cond_w_up", "L0_cond_w_down", "L0_cond_sw_gate", "L0_cond_sw_up", "L0_cond_sw_down", "L1_cond_g_in",
        "L1_cond_null_attn_bias", "L1_cond_Wq", "L1_cond_Wkv", "L1_cond_Wo", "L1_cond_g_out"]


def kernel(**inputs):
    import numpy as _np
    import concourse.bacc as _bacc
    from concourse import mybir as _mybir
    from concourse.bass_utils import run_bass_kernel_spmd as _run

    nc = _bacc.Bacc("TRN2", target_bir_lowering=False, num_devices=1)
    arrays, args = {}, []
    for name in _INS:
        a = _np.ascontiguousarray(inputs[name])
        arrays[f"in_{name}"] = a
        args.append(nc.dram_tensor(f"in_{name}", a.shape, _mybir.dt.from_np(a.dtype), kind="ExternalInput").ap())
    shape = inputs["x"].shape
    args.append(nc.dram_tensor("out_x", shape, _mybir.dt.float32, kind="ExternalOutput").ap())
    moe_then_attention(nc, *args)
    r = _run(nc, [arrays], core_ids=[0])
    return r.results[0]["out_x"]
```
